# Optimizing a Trainium2 kernel written in Bass

```python
import numpy as np
import jax
import jax.numpy as jnp

def _softmax(x, axis=-1):
    return jax.nn.softmax(x, axis=axis)
def _gelu(x):
    return jax.nn.gelu(x, approximate=True)
def _silu(x):
    return jax.nn.silu(x)
def _sigmoid(x):
    return jax.nn.sigmoid(x)
def _layernorm(x, axis=-1, eps=1e-5):
    m = jnp.mean(x, axis=axis, keepdims=True)
    v = jnp.var(x, axis=axis, keepdims=True)
    return (x - m) / jnp.sqrt(v + eps)
def _scatter_add(tgt, idx, src, axis=0):
    return tgt.at[idx].add(src)
def _segment_sum(src, seg, n):
    return jax.ops.segment_sum(src, seg, n)

kernel_name = 'mk_adj_preln_d2_adj_128_b20718'

def setup_inputs(seed: int = 0):
    np.random.seed(seed)
    _w = jnp.asarray
    def _rec_inputs():
        import jax
        import jax.numpy as jnp
        _gk = jax.random.key(seed)
        x = -0.0005207 + 1.001 * jax.random.normal(jax.random.fold_in(_gk, 1), (8192, 128), jnp.float32)
        _a = jax.random.bernoulli(jax.random.fold_in(_gk, 2), 0.000488281, (8192, 8192))
        _a = jnp.logical_or(_a, jnp.swapaxes(_a, -1, -2))
        _a = jnp.logical_or(_a, jnp.eye(8192, dtype=bool))
        _af = _a.astype(jnp.float32)
        adj = _af
        return x, adj
    x, adj = _rec_inputs()
    def _L0_gnn_setup():
        import jax, jax.numpy as jnp
        import numpy as np
        N = 16384
        U = 128
        AVG_DEGREE = 32
        key = jax.random.key(seed)
        kx, ka, kw = jax.random.split(key, 3)
        x = jax.random.normal(kx, (N, U), dtype=jnp.float32)
        adj = (jax.random.uniform(ka, (N, N)) < AVG_DEGREE / N).astype(jnp.float32)
        W = jax.random.normal(kw, (U, U), dtype=jnp.float32) * 0.05
        b = jnp.zeros((U,), dtype=jnp.float32)
        return {'x': x, 'adj': adj, 'W': W, 'b': b}
    _L0_gnn_all = _L0_gnn_setup()
    _L0_gnn_in = {k: v for k, v in _L0_gnn_all.items() if k in ('W', 'b', )}
    del _L0_gnn_all

    def _L1_gnn_setup():
        import jax, jax.numpy as jnp
        import numpy as np
        N = 8192
        D_IN = 128
        D_OUT = 128
        key = jax.random.key(seed)
        k1, k2, k3, k4 = jax.random.split(key, 4)
        x = jax.random.normal(k1, (N, D_IN), dtype=jnp.float32)
        adj = jax.random.uniform(k2, (N, N), dtype=jnp.float32)
        W = jax.random.normal(k3, (D_OUT, D_IN), dtype=jnp.float32) * (1.0 / np.sqrt(D_IN))
        b = jax.random.normal(k4, (D_OUT,), dtype=jnp.float32) * 0.01
        return {'x': x, 'adj': adj, 'W': W, 'b': b}
    _L1_gnn_all = _L1_gnn_setup()
    _L1_gnn_in = {k: v for k, v in _L1_gnn_all.items() if k in ('W', 'b', )}
    del _L1_gnn_all

    return {
        "x": x,
        "adj": adj,
        "L0_gnn_W": _L0_gnn_in["W"],
        "L0_gnn_b": _L0_gnn_in["b"],
        "L1_gnn_W": _L1_gnn_in["W"],
        "L1_gnn_b": _L1_gnn_in["b"],
    }

def reference(x, adj, L0_gnn_W, L0_gnn_b, L1_gnn_W, L1_gnn_b):
    import jax
    import jax.numpy as jnp
    def _L0_gnn_ref(x, adj, W, b):
        import jax, jax.numpy as jnp
        import numpy as np
        N = 16384
        U = 128
        AVG_DEGREE = 32
        adj = jax.lax.stop_gradient(adj)
        neigh1 = adj @ x
        x1 = jax.nn.swish(neigh1 @ W + b)
        neigh2 = adj @ x1
        x2 = jax.nn.swish(neigh2 @ W + b)
        return x2

    def _L1_gnn_ref(x, adj, W, b):
        import jax, jax.numpy as jnp
        import numpy as np
        N = 8192
        D_IN = 128
        D_OUT = 128
        a_hat = adj + jnp.eye(adj.shape[0], dtype=adj.dtype)
        d_inv_sqrt = jnp.sum(a_hat, axis=1) ** (-0.5)
        a_norm = a_hat * d_inv_sqrt[:, None] * d_inv_sqrt[None, :]
        out = a_norm @ x
        out = out @ W.T + b
        return out

    h = jnp.maximum(_layernorm(x, axis=-1), 0.0)
    x = x + _L0_gnn_ref(h, adj, L0_gnn_W, L0_gnn_b)
    h = jnp.maximum(_layernorm(x, axis=-1), 0.0)
    x = x + _L1_gnn_ref(h, adj, L1_gnn_W, L1_gnn_b)
    return x


_drawn_inputs = setup_inputs


def setup_inputs(seed=0):
    import zlib

    import numpy as np

    out = dict(_drawn_inputs(seed))
    spreads = {'L0_gnn_b': (0.0, 0.1)}
    factors = {'L1_gnn_b': 25.821}
    for name, (base, spread) in spreads.items():
        noise = np.random.default_rng([zlib.crc32(name.encode()), seed]).standard_normal(out[name].shape)
        drawn = base * np.exp(spread * noise) if base else spread * noise
        out[name] = jnp.asarray(drawn.astype(out[name].dtype))
    for name, factor in factors.items():
        out[name] = (out[name] * factor).astype(out[name].dtype)
    return out
```

```python
import numpy as np
import concourse.bass as bass
from concourse import mybir
from contextlib import ExitStack

F32 = mybir.dt.float32
I32 = mybir.dt.int32
ALU = mybir.AluOpType
ACT = mybir.ActivationFunctionType
AX = mybir.AxisListType

P = 128
N = 8192
D = 128
NB = N // P
CW = 512
CB = CW // P
NC = N // CW
TB = 4
TC = NB // TB
RING = 4
EPS = 1e-5
RSQRT_STEPS = 14
SCALE_STEPS = 5 + RSQRT_STEPS
MAGIC = float(0x5F3759DF)
HUGE = 3e38


def chain(dve, step, start):
    count = [start]

    def link(ins):
        ins.then_inc(step, 1)
        count[0] = count[0] + 1
        dve.wait_ge(step, count[0])
    return link


def rsqrt(nc, link, v, r, a):
    link(nc.vector.tensor_scalar(r.bitcast(I32), v.bitcast(I32), 1, None, ALU.logical_shift_right))
    link(nc.vector.tensor_scalar(r.bitcast(I32), r.bitcast(I32), -1.0, MAGIC, ALU.mult, ALU.add))
    for _ in range(3):
        link(nc.vector.tensor_tensor(a, r, r, ALU.mult))
        link(nc.vector.tensor_tensor(a, a, v, ALU.mult))
        link(nc.vector.tensor_scalar(a, a, -0.5, 1.5, ALU.mult, ALU.add))
        link(nc.vector.tensor_tensor(r, r, a, ALU.mult))


def norm_scales(nc, link, stats, total, var, rstd, tmp):
    st = stats.rearrange("p (j s) -> p j s", s=6)
    tot = total.rearrange("p (j s) -> p j s", s=2)
    link(nc.vector.tensor_tensor(tot, st[:, :, 1:3], st[:, :, 4:6], ALU.add))
    link(nc.vector.tensor_tensor(tmp, st[:, :, 1], st[:, :, 4], ALU.subtract))
    link(nc.vector.scalar_tensor_tensor(tmp, tmp, 0.25, tmp, ALU.mult, ALU.mult))
    link(nc.vector.scalar_tensor_tensor(var, tot[:, :, 1], 1.0 / D, tmp, ALU.mult, ALU.add))
    link(nc.vector.tensor_scalar(var, var, EPS, None, ALU.add))
    rsqrt(nc, link, var, rstd, tmp)


def program(nc, x, adj, w0, b0, w1t, b1, out):
    adj_t = adj.rearrange("(t p) n -> t p n", p=P)
    x_v = x.rearrange("(j p) d -> p j d", p=P)
    out_v = out.rearrange("(j p) d -> p j d", p=P)
    ctx = ExitStack()
    with ctx:
        def sb(name, shape, dt=F32):
            return ctx.enter_context(nc.sbuf_tensor(name, shape, dt))

        def pb(name):
            return ctx.enter_context(nc.psum_tensor(name, [P, CW], F32))

        def sem(name):
            return ctx.enter_context(nc.semaphore(name))

        xn_dram = nc.dram_tensor("xn_scratch", [N, D], F32, kind="Internal").ap()
        xn_v = xn_dram.rearrange("(j p) d -> p j d", p=P)

        node_a = sb("node_a", [P, NB * D])
        node_b = sb("node_b", [P, NB * D])
        ring = sb("ring", [P, RING * TB * CW])
        w_sb = sb("w_sb", [P, 2 * D])
        b_sb = sb("b_sb", [P, 2 * D])
        ident = sb("ident", [P, P])
        ones = sb("ones", [P, P])
        stats = sb("stats", [P, NB * 6])
        mv = sb("mv", [P, NB * 2])
        var = sb("var", [P, NB])
        rstd = sb("rstd", [P, NB])
        tmp = sb("tmp", [P, NB])
        nmr = sb("nmr", [P, NB])
        deg = sb("deg", [P, NB])
        dinv = sb("dinv", [P, NB])
        degacc = sb("degacc", [P, 2 * CW])
        degtile = sb("degtile", [P, CW])
        own = sb("own", [P, 2 * CW])
        nT = sb("nT", [P, 2 * CW])
        zb = sb("zb", [P, CW])
        sig = sb("sig", [P, CW])
        xch = sb("xch", [P, 2 * CW])
        xnew = sb("xnew", [P, 2 * CW])

        neigh_ps = [pb("neigh0_ps"), pb("neigh1_ps")]
        z_ps = pb("z_ps")
        misc_ps = pb("misc_ps")

        x_in, w_in = [sem(f"x_in{q}") for q in range(4)], sem("w_in")
        tile_in = [sem(f"tile_in{s}") for s in range(RING)]
        consts_set, ident_zero = sem("consts_set"), sem("ident_zero")
        stat_done, scale_step, dinv_step = sem("stat_done"), sem("scale_step"), sem("dinv_step")
        nmr_done = sem("nmr_done")
        h_ready = sem("h_ready")
        tile_mm = sem("tile_mm")
        tile_red = sem("tile_red")
        neigh_done, nT_ready, z_done = sem("neigh_done"), sem("nT_ready"), sem("z_done")
        degacc_done, dcol_done, deg_done, dinv_done = sem("degacc_done"), sem("dcol_done"), sem("deg_done"), sem("dinv_done")
        degstep = sem("degstep")
        zb_ready, sig_ready, node_ready = sem("zb_ready"), sem("sig_ready"), sem("node_ready")
        xch_in = [sem("xch_in0"), sem("xch_in1")]
        own_ready = sem("own_ready")
        xb_ready = sem("xb_ready")
        xn_ready, xn_out = sem("xn_ready"), [sem("xn_out0"), sem("xn_out1")]
        stats_ready = sem("stats_ready")
        out_ready, out_done = sem("out_ready"), [sem("out_done0"), sem("out_done1")]
        sdone = sem("sdone")

        def blocks(buf, first, n):
            return buf[:, bass.ds(first * D, n * D)]

        def b3(ap):
            return ap.rearrange("p (j d) -> p j d", d=D)

        def bias(which):
            return b_sb[:, which * D:(which + 1) * D].unsqueeze(1).to_broadcast([P, CB, D])

        def chunks(eng, body):
            body(0, True)
            with eng.Fori(1, NC // 2) as turn:
                body(turn, False)

        block = ctx.enter_context(nc.Block())

        @block.sync
        def _(sp):
            for q in range(4):
                sp.dma_start(b3(node_b[:, q * 16 * D:(q + 1) * 16 * D]), x_v[:, q * 16:(q + 1) * 16, :]).then_inc(x_in[q], 16)
                if q == 0:
                    sp.dma_start(w_sb[:, 0:D], w0).then_inc(w_in, 16)
                    sp.dma_start(w_sb[:, D:2 * D], w1t).then_inc(w_in, 16)
                    sp.dma_start(b_sb[:, 0:D], b0.to_broadcast([P, D])).then_inc(w_in, 16)
                    sp.dma_start(b_sb[:, D:2 * D], b1.to_broadcast([P, D])).then_inc(w_in, 16)

            def load_pass(p):
                def body(turn, first):
                    for par in range(2):
                        c = turn * 2 + par
                        t = c + NC * p
                        for i in range(TC):
                            g = t * TC + i
                            if not (p == 0 and first and par == 0 and i < RING):
                                sp.wait_ge(tile_mm, g - RING + 1)
                                if p == 0 or (p == 1 and first and par == 0 and i < RING):
                                    sp.wait_ge(tile_red, g - RING + 1)
                            sp.dma_start(ring[:, (i % RING) * TB * CW:(i % RING + 1) * TB * CW],
                                         adj_t[bass.ds(c * TC + i, 1), :, :].rearrange("o p n -> p (o n)")
                                         ).then_inc(tile_in[i % RING], 16)
                chunks(sp, body)
            for p in range(3):
                load_pass(p)

        @block.gpsimd
        def _(pool):
            nc.gpsimd.memset(ident[:, :], 0.0).then_inc(ident_zero, 1)
            pool.wait_ge(ident_zero, 1)
            nc.gpsimd.affine_select(out=ident[:, :], in_=ident[:, :], compare_op=ALU.not_equal, fill=1.0, base=0,
                                    pattern=[[-1, P]], channel_multiplier=1).then_inc(consts_set, 1)
            for p, src in ((1, x_v), (2, xn_v)):
                def body(turn, first):
                    for par in range(2):
                        c = turn * 2 + par
                        if p == 1 and not first:
                            pool.wait_ge(xn_ready, c - 1)
                        if p == 2:
                            pool.wait_ge(*((xn_ready, NC - 1 + par) if first else (xb_ready, c - 1)))
                        if p == 2:
                            for s in range(2):
                                if first and par == 0:
                                    pool.wait_ge(xn_out[s], 16 * NC // 2)
                        pool.dma_start(b3(xch[:, par * CW:(par + 1) * CW]), src[:, bass.ds(c * CB, CB), :]
                                       ).then_inc(xch_in[par], 16)
                        if p == 2:
                            if first:
                                pool.wait_ge(node_ready, 2 * NC)
                            else:
                                pool.wait_ge(neigh_done, c - 1)
                            nc.gpsimd.tensor_copy(own[:, par * CW:(par + 1) * CW], blocks(node_a, c * CB, CB)).then_inc(own_ready, 1)
                chunks(pool, body)

        @block.tensor
        def _(pe):
            pe.wait_ge(consts_set, 2)
            pe.wait_ge(w_in, 64)

            def project(t, par, p, first=False):
                pe.wait_ge(nT_ready, t + 1)
                if not first:
                    pe.wait_ge(zb_ready, t)
                w = w_sb[:, 0:D] if p < 2 else w_sb[:, D:2 * D]
                for b in range(CB):
                    last = nc.tensor.matmul(z_ps[:, b * D:(b + 1) * D], nT[:, par * CW + b * P:par * CW + (b + 1) * P], w,
                                            start=True, stop=True)
                last.then_inc(z_done, 1)
                if p == 0:
                    pe.wait_ge(degacc_done, t + 1)
                    if not first:
                        pe.wait_ge(deg_done, t)
                    for b in range(CB):
                        last = nc.tensor.matmul(misc_ps[:, b:b + 1], degacc[:, par * CW + b * P:par * CW + (b + 1) * P],
                                                ones[:, 0:1], start=True, stop=True)
                    last.then_inc(dcol_done, 1)

            for p in range(3):
                h = node_b if p == 1 else node_a

                def body(turn, first):
                    for par in range(2):
                        c = turn * 2 + par
                        t = c + NC * p
                        for i in range(TC):
                            pe.wait_ge(tile_in[i % RING], 16 * (t * (TC // RING) + i // RING + 1))
                            if p == 0 and first and par == 0 and i % 4 == 0:
                                pe.wait_ge(h_ready, i // 4 + 1)
                            if p > 0 and first and par == 0:
                                pe.wait_ge(node_ready, NC * (p - 1) + i + 1)
                            for q in range(TB):
                                j = i * TB + q
                                rhs = ring[:, ((i % RING) * TB + q) * CW:((i % RING) * TB + q + 1) * CW]
                                last = nc.tensor.matmul(neigh_ps[par][:, :], h[:, j * D:(j + 1) * D], rhs,
                                                        start=(j == 0), stop=(j == NB - 1 and p < 2))
                            last.then_inc(tile_mm, 1)
                            if i == 1 and not (first and par == 0 and p == 0):
                                project(t - 1, 1 - par, p - 1 if first and par == 0 else p, first and p == 0)
                        if p == 2:
                            pe.wait_ge(own_ready, c + 1)
                            for b in range(CB):
                                o = par * CW + b * D
                                last = nc.tensor.matmul(neigh_ps[par][:, b * P:(b + 1) * P], own[:, o:o + D], ident[:, :],
                                                        start=False, stop=(b == CB - 1))
                            last.then_inc(neigh_done, 1)
                chunks(pe, body)
            project(3 * NC - 1, 1, 2)

        @block.scalar
        def _(act):
            for j in range(NB):
                if j % 16 == 0:
                    act.wait_ge(nmr_done, j // 16 + 1)
                last = nc.scalar.activation(node_a[:, j * D:(j + 1) * D], node_b[:, j * D:(j + 1) * D], ACT.Relu,
                                            bias=nmr[:, j:j + 1], scale=rstd[:, j:j + 1])
                if j % 16 == 15:
                    last.then_inc(h_ready, 1)

            def finish(t, c, par, p):
                act.wait_ge(*((neigh_done, c + 1) if p == 2 else (tile_mm, TC * (t + 1))))
                nc.scalar.copy(nT[:, par * CW:(par + 1) * CW], neigh_ps[par][:, :]).then_inc(nT_ready, 1)
                if p < 2:
                    act.wait_ge(zb_ready, t + 1)
                    nc.scalar.activation(sig[:, :], zb[:, :], ACT.Sigmoid).then_inc(sig_ready, 1)
                if p == 1:
                    act.wait_ge(stats_ready, c + 1)
                    for b in range(CB):
                        last = nc.scalar.activation(blocks(node_a, c * CB + b, 1), xnew[:, par * CW + b * D:par * CW + (b + 1) * D],
                                                    ACT.Relu, bias=nmr[:, b:b + 1], scale=rstd[:, b:b + 1])
                    last.then_inc(node_ready, 1)
                    act.wait_ge(xn_ready, c + 1)
                    act.dma_start(xn_v[:, bass.ds(c * CB, CB), :], b3(xnew[:, par * CW:(par + 1) * CW])).then_inc(xn_out[par], 16)
                if p == 2:
                    act.wait_ge(out_ready, c + 1)
                    act.dma_start(out_v[:, bass.ds(c * CB, CB), :], b3(xnew[:, par * CW:(par + 1) * CW])).then_inc(out_done[par], 16)

            for p in range(3):
                def body(turn, first):
                    for par in range(2):
                        c = turn * 2 + par
                        finish(c + NC * p, c, par, p)
                chunks(act, body)
            for par in range(2):
                act.wait_ge(out_done[par], 16 * NC // 2)

        @block.vector
        def _(dve):
            nc.vector.memset(ones[:, :], 1.0).then_inc(consts_set, 1)
            for q in range(4):
                dve.wait_ge(x_in[q], 16)
                for j in range(q * 16, q * 16 + 16):
                    last = nc.vector.bn_stats(stats[:, j * 6:j * 6 + 6], node_b[:, j * D:(j + 1) * D])
                last.then_inc(stat_done, 1)
                dve.wait_ge(stat_done, q + 1)
                s = slice(q * 16, q * 16 + 16)
                norm_scales(nc, chain(dve, scale_step, SCALE_STEPS * q), stats[:, q * 96:q * 96 + 96], mv[:, q * 32:q * 32 + 32],
                            var[:, s], rstd[:, s], tmp[:, s])
                mq = mv[:, q * 32:q * 32 + 32].rearrange("p (j s) -> p j s", s=2)
                nc.vector.scalar_tensor_tensor(nmr[:, s], mq[:, :, 0], -0.5, rstd[:, s], ALU.mult, ALU.mult).then_inc(nmr_done, 1)

            def finish(t, c, par, p, first):
                zb3, z3 = b3(zb[:, :]), b3(z_ps[:, :])
                dve.wait_ge(z_done, t + 1)
                if p == 0:
                    nc.vector.tensor_tensor(zb3, z3, bias(0), ALU.add).then_inc(zb_ready, 1)
                    dve.wait_ge(dcol_done, t + 1)
                    nc.vector.tensor_scalar(deg[:, bass.ds(c * CB, CB)], misc_ps[:, 0:CB], 1.0, None, ALU.add).then_inc(deg_done, 1)
                    dve.wait_ge(sig_ready, t + 1)
                    nc.vector.tensor_tensor(blocks(node_b, c * CB, CB), zb[:, :], sig[:, :], ALU.mult).then_inc(node_ready, 1)
                if p == 1:
                    x_c, xn = xch[:, par * CW:(par + 1) * CW], xnew[:, par * CW:(par + 1) * CW]
                    nc.vector.tensor_tensor(zb3, z3, bias(0), ALU.add).then_inc(zb_ready, 1)
                    dve.wait_ge(sig_ready, t + 1)
                    nc.vector.tensor_tensor(zb[:, :], zb[:, :], sig[:, :], ALU.mult).then_inc(sdone, 1)
                    dve.wait_ge(sdone, t - NC + 1)
                    dve.wait_ge(xch_in[par], 16 * (turn_of(c, par) + 1))
                    if not first:
                        dve.wait_ge(xn_out[par], 16 * turn_of(c, par))
                        dve.wait_ge(node_ready, NC + c - 1)
                    nc.vector.tensor_tensor(xn, x_c, zb[:, :], ALU.add).then_inc(xn_ready, 1)
                    dve.wait_ge(xn_ready, c + 1)
                    for b in range(CB):
                        last = nc.vector.bn_stats(stats[:, b * 6:b * 6 + 6], xn[:, b * D:(b + 1) * D])
                    last.then_inc(stat_done, 1)
                    dve.wait_ge(stat_done, 4 + c + 1)
                    if not (first and par == 0):
                        dve.wait_ge(node_ready, NC + c)
                    norm_scales(nc, chain(dve, scale_step, (c + 4) * SCALE_STEPS), stats[:, 0:6 * CB], mv[:, 0:2 * CB],
                                var[:, 0:CB], rstd[:, 0:CB], tmp[:, 0:CB])
                    mq = mv[:, 0:2 * CB].rearrange("p (j s) -> p j s", s=2)
                    nc.vector.tensor_tensor(rstd[:, 0:CB], rstd[:, 0:CB], dinv[:, bass.ds(c * CB, CB)], ALU.mult).then_inc(nmr_done, 1)
                    dve.wait_ge(nmr_done, 4 + c + 1)
                    nc.vector.scalar_tensor_tensor(nmr[:, 0:CB], mq[:, :, 0], -0.5, rstd[:, 0:CB], ALU.mult, ALU.mult).then_inc(stats_ready, 1)
                if p == 2:
                    x_c, o = xch[:, par * CW:(par + 1) * CW], xnew[:, par * CW:(par + 1) * CW]
                    dd = dinv[:, bass.ds(c * CB, CB)].unsqueeze(2).to_broadcast([P, CB, D])
                    nc.vector.tensor_tensor(zb3, z3, dd, ALU.mult).then_inc(zb_ready, 1)
                    dve.wait_ge(zb_ready, t + 1)
                    dve.wait_ge(xch_in[par], 16 * (NC // 2 + turn_of(c, par) + 1))
                    if first:
                        dve.wait_ge(xn_out[par], 16 * (NC // 2))
                    else:
                        dve.wait_ge(out_done[par], 16 * turn_of(c, par))
                    nc.vector.tensor_tensor(b3(o), b3(x_c), bias(1), ALU.add).then_inc(xb_ready, 1)
                    dve.wait_ge(xb_ready, c + 1)
                    nc.vector.tensor_tensor(o, o, zb[:, :], ALU.add).then_inc(out_ready, 1)

            def turn_of(c, par):
                return turn_now[0]

            turn_now = [0]
            for p in range(3):
                def body(turn, first):
                    turn_now[0] = turn
                    for par in range(2):
                        c = turn * 2 + par
                        t = c + NC * p
                        if p == 0:
                            acc = degacc[:, par * CW:(par + 1) * CW]
                            for i in range(TC):
                                g = t * TC + i
                                dve.wait_ge(tile_in[i % RING], 16 * (t * (TC // RING) + i // RING + 1))
                                if i == 0 and not first:
                                    dve.wait_ge(dcol_done, t - 1)
                                til = ring[:, (i % RING) * TB * CW:(i % RING + 1) * TB * CW].rearrange("p (q n) -> p n q", q=TB)
                                nc.vector.tensor_reduce(acc if i == 0 else degtile[:, :], til, AX.X, ALU.add).then_inc(tile_red, 1)
                                dve.wait_ge(tile_red, g + 1)
                                if i > 0:
                                    last = nc.vector.tensor_tensor(acc, acc, degtile[:, :], ALU.add)
                                    last.then_inc(degacc_done if i == TC - 1 else degstep, 1)
                                    if i < TC - 1:
                                        dve.wait_ge(degstep, t * (TC - 2) + i)
                        finish(t, c, par, p, first)
                chunks(dve, body)
                if p == 0:
                    dve.wait_ge(deg_done, NC)
                    rsqrt(nc, chain(dve, dinv_step, 0), deg[:, :], dinv[:, :], tmp[:, :])
                    nc.vector.tensor_tensor(dinv[:, :], dinv[:, :], deg[:, :], ALU.mult).then_inc(dinv_done, 1)
                    dve.wait_ge(dinv_done, 1)
                    nc.vector.reciprocal(dinv[:, :], dinv[:, :]).then_inc(dinv_done, 1)
                    nc.vector.tensor_scalar(tmp[:, :], deg[:, :], 0.0, HUGE, ALU.is_lt, ALU.mult).then_inc(dinv_done, 1)
                    dve.wait_ge(dinv_done, 3)
                    nc.vector.tensor_scalar(tmp[:, :], tmp[:, :], HUGE, None, ALU.mult).then_inc(dinv_done, 1)
                    dve.wait_ge(dinv_done, 4)
                    nc.vector.tensor_tensor(tmp[:, :], tmp[:, :], tmp[:, :], ALU.subtract).then_inc(dinv_done, 1)
                    dve.wait_ge(dinv_done, 5)
                    nc.vector.tensor_tensor(dinv[:, :], dinv[:, :], tmp[:, :], ALU.add).then_inc(dinv_done, 1)
                    dve.wait_ge(dinv_done, 6)


def kernel(x, adj, L0_gnn_W, L0_gnn_b, L1_gnn_W, L1_gnn_b):
    import concourse.bacc as bacc
    from concourse.bass_utils import run_bass_kernel_spmd

    nc = bacc.Bacc("TRN2", target_bir_lowering=False, num_devices=1)
    tiles = np.asarray(adj).reshape(NC, CW, TC, TB, P).transpose(0, 2, 4, 3, 1)
    arrays = {
        "x": np.ascontiguousarray(x),
        "adj": np.ascontiguousarray(tiles).reshape(NC * TC * P, TB * CW),
        "w0": np.ascontiguousarray(L0_gnn_W),
        "b0": np.ascontiguousarray(L0_gnn_b).reshape(1, D),
        "w1t": np.ascontiguousarray(np.asarray(L1_gnn_W).T),
        "b1": np.ascontiguousarray(L1_gnn_b).reshape(1, D),
    }
    args = [nc.dram_tensor(k, a.shape, mybir.dt.from_np(a.dtype), kind="ExternalInput").ap() for k, a in arrays.items()]
    out = nc.dram_tensor("out", (N, D), F32, kind="ExternalOutput").ap()
    program(nc, *args, out)
    r = run_bass_kernel_spmd(nc, [arrays], core_ids=[0])
    return r.results[0]["out"]
```

```python
import numpy as np
import concourse.bass as bass
from concourse import mybir
from contextlib import ExitStack

F32 = mybir.dt.float32
I32 = mybir.dt.int32
ALU = mybir.AluOpType
ACT = mybir.ActivationFunctionType
AX = mybir.AxisListType

P = 128
N = 8192
D = 128
NB = N // P
CW = 512
CB = CW // P
NC = N // CW
TB = 4
TC = NB // TB
RING = 4
EPS = 1e-5
RSQRT_STEPS = 14
SCALE_STEPS = 5 + RSQRT_STEPS
MAGIC = float(0x5F3759DF)
HUGE = 3e38
F16 = mybir.dt.float16
F8 = mybir.dt.float8e4
U8 = mybir.dt.uint8
U32 = mybir.dt.uint32
UB = 2 * TB
UC = NB // UB
WORDS = CW // 4
GB = 2
GC = UC // GB
H_SCALE = 1024.0
LO = 2048.0
ONE = 2.0
ONE_BYTE = 0x40
ONE_WORD = 0x40404040
BIT = {0: 1, 4: 0, 2: 3, 6: 2, 1: 5, 5: 4, 3: 7, 7: 6}
SUM_BOUND = 93000.0


def chain(dve, step, start):
    count = [start]

    def link(ins):
        ins.then_inc(step, 1)
        count[0] = count[0] + 1
        dve.wait_ge(step, count[0])
    return link


def rsqrt(nc, link, v, r, a):
    link(nc.vector.tensor_scalar(r.bitcast(I32), v.bitcast(I32), 1, None, ALU.logical_shift_right))
    link(nc.vector.tensor_scalar(r.bitcast(I32), r.bitcast(I32), -1.0, MAGIC, ALU.mult, ALU.add))
    for _ in range(3):
        link(nc.vector.tensor_tensor(a, r, r, ALU.mult))
        link(nc.vector.tensor_tensor(a, a, v, ALU.mult))
        link(nc.vector.tensor_scalar(a, a, -0.5, 1.5, ALU.mult, ALU.add))
        link(nc.vector.tensor_tensor(r, r, a, ALU.mult))


def norm_scales(nc, link, stats, total, var, rstd, tmp):
    st = stats.rearrange("p (j s) -> p j s", s=6)
    tot = total.rearrange("p (j s) -> p j s", s=2)
    link(nc.vector.tensor_tensor(tot, st[:, :, 1:3], st[:, :, 4:6], ALU.add))
    link(nc.vector.tensor_tensor(tmp, st[:, :, 1], st[:, :, 4], ALU.subtract))
    link(nc.vector.scalar_tensor_tensor(tmp, tmp, 0.25, tmp, ALU.mult, ALU.mult))
    link(nc.vector.scalar_tensor_tensor(var, tot[:, :, 1], 1.0 / D, tmp, ALU.mult, ALU.add))
    link(nc.vector.tensor_scalar(var, var, EPS, None, ALU.add))
    rsqrt(nc, link, var, rstd, tmp)



class Signals:

    def __init__(self, sem, path):
        self.nT_ready = sem(path + "nT_ready")
        self.z_done = sem(path + "z_done")
        self.zb_ready = sem(path + "zb_ready")
        self.sig_ready = sem(path + "sig_ready")
        self.node_ready = sem(path + "node_ready")
        self.gated = sem(path + "gated")
        self.xch_in = [sem(path + "xch_in0"), sem(path + "xch_in1")]
        self.xn_ready = sem(path + "xn_ready")
        self.xn_out = [sem(path + "xn_out0"), sem(path + "xn_out1")]
        self.stat_done = sem(path + "stat_done")
        self.scale_step = sem(path + "scale_step")
        self.rs_done = sem(path + "rs_done")
        self.stats_ready = sem(path + "stats_ready")
        self.xb_ready = sem(path + "xb_ready")
        self.out_ready = sem(path + "out_ready")
        self.out_done = [sem(path + "out_done0"), sem(path + "out_done1")]
        self.neigh_done = sem(path + "neigh_done")
        self.ln_stat = sem(path + "ln_stat")
        self.ln_step = sem(path + "ln_step")
        self.ln_ready = sem(path + "ln_ready")
        self.h_ready = sem(path + "h_ready")
        self.deg_done = sem(path + "deg_done")
        self.dcol_done = sem(path + "dcol_done")
        self.dinv_step = sem(path + "dinv_step")


def program(nc, x, adj, w0, b0, w1t, b1, out):
    adj_t = adj.rearrange("(t p) n -> t p n", p=P)
    x_v = x.rearrange("(j p) d -> p j d", p=P)
    out_v = out.rearrange("(j p) d -> p j d", p=P)
    ctx = ExitStack()
    with ctx:
        def sb(name, shape, dt=F32):
            return ctx.enter_context(nc.sbuf_tensor(name, shape, dt))

        def pb(name):
            return ctx.enter_context(nc.psum_tensor(name, [P, CW], F32))

        def sem(name):
            return ctx.enter_context(nc.semaphore(name))

        xn_dram = nc.dram_tensor("xn_scratch", [N, D], F32, kind="Internal").ap()
        xn_v = xn_dram.rearrange("(j p) d -> p j d", p=P)

        node_a = sb("node_a", [P, NB * D])
        node_b = sb("node_b", [P, NB * D])
        ring = sb("ring", [P, RING * TB * CW])
        bits = sb("bits", [P, NC * UC * WORDS], U32)
        marks = sb("marks", [P, 2 * UB * CW], U8)
        unused = sb("unused", [P, 2 * TB * CW], U8)
        w_sb = sb("w_sb", [P, 2 * D])
        b_sb = sb("b_sb", [P, 2 * D])
        ident = sb("ident", [P, P])
        ident16 = sb("ident16", [P, P], F16)
        ones = sb("ones", [P, P])
        half16 = sb("half16", [P, P], F16)
        first_row = sb("first_row", [P, 1])
        stats = sb("stats", [P, NB * 6])
        mv = sb("mv", [P, NB * 2])
        var = sb("var", [P, NB])
        rstd = sb("rstd", [P, NB])
        tmp = sb("tmp", [P, NB])
        nmr = sb("nmr", [P, NB])
        deg = sb("deg", [P, NB])
        dinv = sb("dinv", [P, NB])
        nz_count = sb("nz_count", [P, NC * TC])
        nz_chunk = sb("nz_chunk", [P, NC])
        one_count = sb("one_count", [P, NC])
        differ = sb("differ", [P, NC])
        flag_f = sb("flag_f", [P, 1])
        flag = sb("flag", [P, 1], I32)
        s_row = sb("s_row", [P, D])
        alpha1 = sb("alpha1", [P, 2])
        nT = sb("nT", [P, 2 * CW])
        lo_sum = sb("lo_sum", [P, CW])
        zb = sb("zb", [P, CW])
        sig = sb("sig", [P, CW])
        y = sb("y", [P, CW])
        rest = sb("rest", [P, CW])
        deg_sb = sb("deg_sb", [P, CW])
        xch = sb("xch", [P, 2 * CW])
        xnew = sb("xnew", [P, 2 * CW])
        pack4 = xnew[:, 0:4 * WORDS].bitcast(U32)
        pack2 = xch[:, 0:2 * WORDS].bitcast(U32)
        wsq, bound, wtmp = xch[:, CW:CW + D], xnew[:, CW:CW + D], xnew[:, CW + D:CW + 2 * D]
        scratch = marks[:, :].bitcast(F32)
        degacc, own = scratch[:, 0:2 * CW], scratch[:, 2 * CW:4 * CW]
        degtile = deg_sb[:, :]

        hi_ps = [pb("hi0_ps"), pb("hi1_ps")]
        lo_ps = [pb("lo0_ps"), pb("lo1_ps")]
        deg_ps = [pb("deg0_ps"), pb("deg1_ps")]
        z_ps = pb("z_ps")
        misc_ps = pb("misc_ps")

        S = Signals(sem, "")
        G = Signals(sem, "g_")
        x_in = [sem(f"x_in{u}") for u in range(UC)]
        w_in = sem("w_in")
        tile_in = [sem(f"tile_in{s}") for s in range(RING)]
        ones_set, ident_zero, ident_set, ident16_set = sem("ones_set"), sem("ident_zero"), sem("ident_set"), sem("ident16_set")
        row_zero = sem("row_zero")
        hy_ready, hhi_ready, hrest_ready = sem("hy_ready"), sem("hhi_ready"), sem("hrest_ready")
        marked, counted, unit_mm = sem("marked"), sem("counted"), sem("unit_mm")
        pack4_ready, pack2_ready, bits_ready = sem("pack4_ready"), sem("pack2_ready"), sem("bits_ready")
        lo_ready, deg_sb_ready = sem("lo_ready"), sem("deg_sb_ready")
        ys_ready, y_ready, hi_ready, rest_ready = sem("ys_ready"), sem("y_ready"), sem("hi_ready"), sem("rest_ready")
        wsq_ready, wsum_done, bound_step, s_ready, s_col_done, alpha_step = (
            sem("wsq_ready"), sem("wsum_done"), sem("bound_step"), sem("s_ready"), sem("s_col_done"), sem("alpha_step"))
        nz_ready, nz_total, flag_step, flag_ready = sem("nz_ready"), sem("nz_total"), sem("flag_step"), sem("flag_ready")
        settled = sem("settled")
        unpacked, slot_used = sem("unpacked"), sem("slot_used")
        g_x_in = [sem(f"g_x_in{q}") for q in range(4)]
        g_tile_in = [sem(f"g_tile_in{s}") for s in range(RING)]
        g_tile_mm, g_tile_red, g_degstep, g_degacc_done, g_own_ready, g_dinv_done = (
            sem("g_tile_mm"), sem("g_tile_red"), sem("g_degstep"), sem("g_degacc_done"), sem("g_own_ready"), sem("g_dinv_done"))

        node_a16, node_b16 = node_a[:, :].bitcast(F16), node_b[:, :].bitcast(F16)

        def blocks(buf, first, n):
            return buf[:, bass.ds(first * D, n * D)]

        def lo_blocks(buf, first, n):
            return buf[:, bass.ds(first * D + NB * D, n * D)]

        def b3(ap):
            return ap.rearrange("p (j d) -> p j d", d=D)

        def bias(which):
            return b_sb[:, which * D:(which + 1) * D].unsqueeze(1).to_broadcast([P, CB, D])

        def half(buf, par):
            return buf[:, par * CW:(par + 1) * CW]

        def slot(i):
            return ring[:, (i % RING) * TB * CW:(i % RING + 1) * TB * CW]

        def chunks(eng, body, peel_last=False):
            body(0, True)
            with eng.Fori(1, NC // 2 - peel_last) as turn:
                body(turn, False)
            if peel_last:
                body(NC // 2 - 1, False)

        def branch(eng, fast, general):
            eng.wait_ge(flag_ready, 1)
            found = eng.value_load(flag[0:1, 0:1], min_val=0, max_val=1)
            with eng.If(found == 0):
                fast()
            with eng.Else():
                general()


        def load_chunks(pool, S, general):
            for p, src in ((1, x_v), (2, xn_v)):
                def body(turn, first):
                    for par in range(2):
                        c = turn * 2 + par
                        if p == 1 and not first:
                            pool.wait_ge(S.xn_ready, c - 1)
                        if p == 2 and first:
                            pool.wait_ge(S.xn_ready, NC - 1 + par)
                        if p == 2 and not first:
                            pool.wait_ge(S.xb_ready, c - 1)
                        if p == 2 and first and par == 0:
                            pool.wait_ge(S.xn_out[0], 16 * NC // 2)
                            pool.wait_ge(S.xn_out[1], 16 * NC // 2)
                        pool.dma_start(b3(half(xch, par)), src[:, bass.ds(c * CB, CB), :]).then_inc(S.xch_in[par], 16)
                        if p == 2 and general:
                            if first:
                                pool.wait_ge(S.node_ready, 2 * NC)
                            else:
                                pool.wait_ge(S.neigh_done, c - 1)
                            nc.gpsimd.tensor_copy(half(own, par), blocks(node_a, c * CB, CB)).then_inc(g_own_ready, 1)
                chunks(pool, body)

        def project_z(pe, S, t, par, p, first):
            pe.wait_ge(S.nT_ready, t + 1)
            if not first:
                pe.wait_ge(S.zb_ready, t)
            w = w_sb[:, 0:D] if p < 2 else w_sb[:, D:2 * D]
            for b in range(CB):
                last = nc.tensor.matmul(z_ps[:, b * D:(b + 1) * D], nT[:, par * CW + b * P:par * CW + (b + 1) * P], w,
                                        start=True, stop=True)
            last.then_inc(S.z_done, 1)

        def first_norm(dve, S, arrived, part, n, scale):
            a, s = part * n, slice(part * n, part * n + n)
            dve.wait_ge(arrived, 16)
            for j in range(a, a + n):
                last = nc.vector.bn_stats(stats[:, j * 6:j * 6 + 6], node_b[:, j * D:(j + 1) * D])
            last.then_inc(S.ln_stat, 1)
            dve.wait_ge(S.ln_stat, part + 1)
            link = chain(dve, S.ln_step, (SCALE_STEPS + 1) * part)
            norm_scales(nc, link, stats[:, a * 6:(a + n) * 6], mv[:, a * 2:(a + n) * 2], var[:, s], rstd[:, s], tmp[:, s])
            link(nc.vector.tensor_scalar(rstd[:, s], rstd[:, s], scale, None, ALU.mult))
            twice_mean = mv[:, a * 2:(a + n) * 2].rearrange("p (j s) -> p j s", s=2)[:, :, 0]
            nc.vector.scalar_tensor_tensor(nmr[:, s], twice_mean, -0.5, rstd[:, s], ALU.mult, ALU.mult).then_inc(S.ln_ready, 1)

        def relu_blocks(act, part, n, out_of):
            for j in range(part * n, part * n + n):
                last = nc.scalar.activation(out_of(j), node_b[:, j * D:(j + 1) * D], ACT.Relu,
                                            bias=nmr[:, j:j + 1], scale=rstd[:, j:j + 1])
            return last

        def finish_dve(dve, S, turn, par, p, first, split):
            c = turn * 2 + par
            t = c + NC * p
            if split:
                dve.wait_ge(lo_ready, t + 1)
                nc.vector.scalar_tensor_tensor(half(nT, par), hi_ps[par][:, :], alpha1[:, 0:1] if p == 1 else 1 / (ONE * H_SCALE),
                                               lo_sum[:, :], ALU.mult, ALU.add).then_inc(S.nT_ready, 1)
            zb3, z3, x_c, xn = b3(zb[:, :]), b3(z_ps[:, :]), half(xch, par), half(xnew, par)
            dve.wait_ge(S.z_done, t + 1)
            if p == 1:
                nc.vector.tensor_tensor(zb3, z3, bias(0), ALU.add).then_inc(S.zb_ready, 1)
                dve.wait_ge(S.sig_ready, t + 1)
                nc.vector.tensor_tensor(zb[:, :], zb[:, :], sig[:, :], ALU.mult).then_inc(S.gated, 1)
                dve.wait_ge(S.gated, c + 1)
                dve.wait_ge(S.xch_in[par], 16 * turn + 16)
                if not first:
                    dve.wait_ge(S.xn_out[par], 16 * turn)
                nc.vector.tensor_tensor(xn, x_c, zb[:, :], ALU.add).then_inc(S.xn_ready, 1)
                dve.wait_ge(S.xn_ready, c + 1)
                for b in range(CB):
                    last = nc.vector.bn_stats(stats[:, b * 6:b * 6 + 6], xn[:, b * D:(b + 1) * D])
                last.then_inc(S.stat_done, 1)
                dve.wait_ge(S.stat_done, c + 1)
                if not (first and par == 0):
                    dve.wait_ge(y_ready if split else S.node_ready, t)
                norm_scales(nc, chain(dve, S.scale_step, c * SCALE_STEPS), stats[:, 0:6 * CB], mv[:, 0:2 * CB],
                            var[:, 0:CB], rstd[:, 0:CB], tmp[:, 0:CB])
                nc.vector.scalar_tensor_tensor(rstd[:, 0:CB], rstd[:, 0:CB], H_SCALE if split else 1.0,
                                               dinv[:, bass.ds(c * CB, CB)], ALU.mult, ALU.mult).then_inc(S.rs_done, 1)
                dve.wait_ge(S.rs_done, c + 1)
                twice_mean = mv[:, 0:2 * CB].rearrange("p (j s) -> p j s", s=2)[:, :, 0]
                nc.vector.scalar_tensor_tensor(nmr[:, 0:CB], twice_mean, -0.5, rstd[:, 0:CB], ALU.mult, ALU.mult).then_inc(S.stats_ready, 1)
                if split:
                    take_rest(dve, t, c, node_a16)
            if p == 2:
                dd = dinv[:, bass.ds(c * CB, CB)].unsqueeze(2).to_broadcast([P, CB, D])
                nc.vector.tensor_tensor(zb3, z3, dd, ALU.mult).then_inc(S.zb_ready, 1)
                dve.wait_ge(S.zb_ready, t + 1)
                dve.wait_ge(S.xch_in[par], 16 * (NC // 2 + turn + 1))
                if first:
                    dve.wait_ge(S.xn_out[par], 16 * (NC // 2))
                else:
                    dve.wait_ge(S.out_done[par], 16 * turn)
                nc.vector.tensor_tensor(b3(xn), b3(x_c), bias(1), ALU.add).then_inc(S.xb_ready, 1)
                dve.wait_ge(S.xb_ready, c + 1)
                nc.vector.tensor_tensor(xn, xn, zb[:, :], ALU.add).then_inc(S.out_ready, 1)

        def finish_act(act, S, turn, par, p, first, split):
            c = turn * 2 + par
            t = c + NC * p
            if p == 2:
                act.wait_ge(S.neigh_done, c + 1)
            elif split:
                act.wait_ge(slot_used, (c + 1) * GC)
            else:
                act.wait_ge(g_tile_mm, TC * (t + 1))
            if split:
                act.wait_ge(S.nT_ready, t)
                scale = alpha1[:, 1:2] if p == 1 else 1 / (ONE * H_SCALE * LO)
                nc.scalar.activation(lo_sum[:, :], lo_ps[par][:, :], ACT.Identity, scale=scale).then_inc(lo_ready, 1)
            else:
                nc.scalar.copy(half(nT, par), hi_ps[par][:, :]).then_inc(S.nT_ready, 1)
            if p < 2:
                act.wait_ge(S.zb_ready, t + 1)
                nc.scalar.activation(sig[:, :], zb[:, :], ACT.Sigmoid).then_inc(S.sig_ready, 1)
            if p == 1:
                act.wait_ge(S.stats_ready, c + 1)
                if split:
                    act.wait_ge(rest_ready, t)
                for b in range(CB):
                    to = y[:, b * D:(b + 1) * D] if split else blocks(node_a, c * CB + b, 1)
                    last = nc.scalar.activation(to, xnew[:, par * CW + b * D:par * CW + (b + 1) * D],
                                                ACT.Relu, bias=nmr[:, b:b + 1], scale=rstd[:, b:b + 1])
                last.then_inc(y_ready if split else S.node_ready, 1)
                if split:
                    high_part(act, t, c, node_a16)
                    low_part(act, S, t, c, node_a16)
                act.wait_ge(S.xn_ready, c + 1)
                act.dma_start(xn_v[:, bass.ds(c * CB, CB), :], b3(half(xnew, par))).then_inc(S.xn_out[par], 16)
            if p == 2:
                act.wait_ge(S.out_ready, c + 1)
                act.dma_start(out_v[:, bass.ds(c * CB, CB), :], b3(half(xnew, par))).then_inc(S.out_done[par], 16)

        def high_part(act, t, c, node):
            act.wait_ge(y_ready, t + 1)
            nc.scalar.copy(blocks(node, c * CB, CB), y[:, :]).then_inc(hi_ready, 1)

        def take_rest(dve, t, c, node, very_first=False):
            dve.wait_ge(hi_ready, t + 1)
            if not very_first:
                dve.wait_ge(S.node_ready, t)
            nc.vector.tensor_tensor(rest[:, :], y[:, :], blocks(node, c * CB, CB), ALU.subtract).then_inc(rest_ready, 1)

        def low_part(act, S, t, c, node):
            act.wait_ge(rest_ready, t + 1)
            nc.scalar.mul(lo_blocks(node, c * CB, CB), rest[:, :], LO).then_inc(S.node_ready, 1)

        def store_end(act, S):
            for par in range(2):
                act.wait_ge(S.out_done[par], 16 * NC // 2)

        block = ctx.enter_context(nc.Block())

        @block.sync
        def _(sp):
            sp.dma_start(w_sb[:, 0:D], w0).then_inc(w_in, 16)
            sp.dma_start(w_sb[:, D:2 * D], w1t).then_inc(w_in, 16)
            sp.dma_start(b_sb[:, 0:D], b0.to_broadcast([P, D])).then_inc(w_in, 16)
            sp.dma_start(b_sb[:, D:2 * D], b1.to_broadcast([P, D])).then_inc(w_in, 16)

            def load_x(part, n, arrived):
                s = slice(part * n, part * n + n)
                sp.dma_start(b3(node_b[:, part * n * D:(part + 1) * n * D]), x_v[:, s, :]).then_inc(arrived, 16)

            def first_pass(turn, first):
                for par in range(2):
                    c = turn * 2 + par
                    for i in range(TC):
                        g = c * TC + i
                        if first and par == 0 and i % 2 == 0:
                            load_x(i // 2, UB, x_in[i // 2])
                        if not (first and par == 0 and i < RING):
                            sp.wait_ge(marked, g - RING + 1)
                            sp.wait_ge(counted, g - RING + 1)
                        sp.dma_start(slot(i), adj_t[bass.ds(g, 1), :, :].rearrange("o p n -> p (o n)")).then_inc(tile_in[i % RING], 16)
            chunks(sp, first_pass)

            def general():
                for q in range(4):
                    load_x(q, 16, g_x_in[q])
                for p in range(3):
                    def body(turn, first):
                        for par in range(2):
                            c = turn * 2 + par
                            for i in range(TC):
                                g = c * TC + i + NC * TC * p
                                if not (p == 0 and first and par == 0 and i < RING):
                                    sp.wait_ge(g_tile_mm, g - RING + 1)
                                    if p == 0 or (p == 1 and first and par == 0 and i < RING):
                                        sp.wait_ge(g_tile_red, g - RING + 1)
                                sp.dma_start(slot(i), adj_t[bass.ds(c * TC + i, 1), :, :].rearrange("o p n -> p (o n)")
                                             ).then_inc(g_tile_in[i % RING], 16)
                    chunks(sp, body)

            branch(sp, lambda: None, general)

        @block.gpsimd
        def _(pool):
            nc.gpsimd.memset(ident[:, :], 0.0).then_inc(ident_zero, 1)
            pool.wait_ge(ident_zero, 1)
            nc.gpsimd.affine_select(out=ident[:, :], in_=ident[:, :], compare_op=ALU.not_equal, fill=1.0, base=0,
                                    pattern=[[-1, P]], channel_multiplier=1).then_inc(ident_set, 1)
            pool.wait_ge(ident_set, 1)
            nc.gpsimd.tensor_scalar(ident16[:, :], ident[:, :], ONE, 0.0, ALU.mult, ALU.add).then_inc(ident16_set, 1)
            for u in range(UC):
                pool.wait_ge(hhi_ready, u + 1)
                a, b = u * UB * D, (u + 1) * UB * D
                nc.gpsimd.tensor_tensor(node_b[:, a:b], node_b[:, a:b], node_a16[:, a:b], ALU.subtract).then_inc(hrest_ready, 1)
            branch(pool, lambda: load_chunks(pool, S, False), lambda: load_chunks(pool, G, True))

        @block.tensor
        def _(pe):
            pe.wait_ge(ones_set, 3)
            pe.wait_ge(ident_set, 1)
            pe.wait_ge(w_in, 64)

            def settle():
                pe.sem_inc(settled, 1)

            def project_first(t, par, first):
                project_z(pe, S, t, par, 0, first)
                pe.wait_ge(deg_sb_ready, t + 1)
                if not first:
                    pe.wait_ge(S.deg_done, t)
                for b in range(CB):
                    last = nc.tensor.matmul(misc_ps[:, b:b + 1], deg_sb[:, b * P:(b + 1) * P], first_row[:, :], start=True, stop=True)
                last.then_inc(S.dcol_done, 1)

            def first_pass(turn, first):
                for par in range(2):
                    c = turn * 2 + par
                    for u in range(UC):
                        if first and par == 0:
                            pe.wait_ge(S.h_ready, u + 1)
                        for i in range(UB):
                            j = u * UB + i
                            if i % TB == 0:
                                pe.wait_ge(marked, c * TC + 2 * u + i // TB + 1)
                                settle()
                            m = marks[:, ((u % 2) * UB + i) * CW:((u % 2) * UB + i + 1) * CW].bitcast(F8)
                            ends = dict(start=(j == 0), stop=(j == NB - 1))
                            nc.tensor.matmul(hi_ps[par][:, :], node_a16[:, j * D:(j + 1) * D], m, **ends)
                            nc.tensor.matmul(lo_ps[par][:, :], node_a16[:, (NB + j) * D:(NB + j + 1) * D], m, **ends)
                            last = nc.tensor.matmul(deg_ps[par][:, :], half16[:, :], m, **ends)
                        last.then_inc(unit_mm, 1)
                        if u == 1 and not (first and par == 0):
                            project_first(c - 1, 1 - par, first)
                    if first and par == 0:
                        pe.wait_ge(wsq_ready, 1)
                        nc.tensor.matmul(z_ps[:, 0:D], ones[:, :], wsq, start=True, stop=True).then_inc(wsum_done, 1)
                        pe.wait_ge(s_ready, 1)
                        nc.tensor.matmul(misc_ps[:, 0:1], s_row[:, :], first_row[:, :], start=True, stop=True).then_inc(s_col_done, 1)
                        pe.wait_ge(alpha_step, 1)
            chunks(pe, first_pass)
            pe.wait_ge(nz_ready, 1)
            pe.wait_ge(S.deg_done, NC - 1)
            nc.tensor.matmul(misc_ps[:, 0:NC], ones[:, :], nz_chunk[:, :], start=True, stop=True).then_inc(nz_total, 1)

            def fast():
                pe.wait_ge(ident16_set, 1)
                for p in (1, 2):
                    node = node_b16 if p == 1 else node_a16

                    def body(turn, first):
                        for par in range(2):
                            c = turn * 2 + par
                            for gq in range(GC):
                                pe.wait_ge(unpacked, (c + NC * (p - 1)) * GC + gq + 1)
                                settle()
                                for i in range(GB * UB):
                                    j = gq * GB * UB + i
                                    if first and par == 0 and j % CB == 0:
                                        pe.wait_ge(S.node_ready, NC * (p - 1) + j // CB + 1)
                                    m = slot(gq)[:, i * WORDS:(i + 1) * WORDS].bitcast(F8)
                                    ends = dict(start=(j == 0), stop=(j == NB - 1 and p == 1))
                                    nc.tensor.matmul(hi_ps[par][:, :], node[:, j * D:(j + 1) * D], m, **ends)
                                    last = nc.tensor.matmul(lo_ps[par][:, :], node[:, (NB + j) * D:(NB + j + 1) * D], m, **ends)
                                    if gq == 0 and i == GB * UB - 1 - UB // 2:
                                        if first and par == 0 and p == 1:
                                            project_first(NC - 1, 1, False)
                                        else:
                                            project_z(pe, S, c - 1 + NC * p, 1 - par, p - 1 if first and par == 0 else p, False)
                                last.then_inc(slot_used, 1)
                            if p == 2:
                                for b in range(CB):
                                    cols = slice(b * P, (b + 1) * P)
                                    nc.tensor.matmul(hi_ps[par][:, cols], blocks(node, c * CB + b, 1), ident16[:, :], start=False, stop=(b == CB - 1))
                                    last = nc.tensor.matmul(lo_ps[par][:, cols], lo_blocks(node, c * CB + b, 1), ident16[:, :],
                                                            start=False, stop=(b == CB - 1))
                                last.then_inc(S.neigh_done, 1)
                    chunks(pe, body)
                project_z(pe, S, 3 * NC - 1, 1, 2, False)

            def general():
                def project(t, par, p, first):
                    project_z(pe, G, t, par, p, first)
                    if p == 0:
                        pe.wait_ge(g_degacc_done, t + 1)
                        if not first:
                            pe.wait_ge(G.deg_done, t)
                        for b in range(CB):
                            last = nc.tensor.matmul(misc_ps[:, b:b + 1], degacc[:, par * CW + b * P:par * CW + (b + 1) * P],
                                                    ones[:, 0:1], start=True, stop=True)
                        last.then_inc(G.dcol_done, 1)

                for p in range(3):
                    h = node_b if p == 1 else node_a

                    def body(turn, first):
                        for par in range(2):
                            c = turn * 2 + par
                            t = c + NC * p
                            for i in range(TC):
                                pe.wait_ge(g_tile_in[i % RING], 16 * (t * (TC // RING) + i // RING + 1))
                                if p == 0 and first and par == 0 and i % 4 == 0:
                                    pe.wait_ge(G.h_ready, i // 4 + 1)
                                if p > 0 and first and par == 0:
                                    pe.wait_ge(G.node_ready, NC * (p - 1) + i + 1)
                                for q in range(TB):
                                    j = i * TB + q
                                    last = nc.tensor.matmul(hi_ps[par][:, :], h[:, j * D:(j + 1) * D], slot(i)[:, q * CW:(q + 1) * CW],
                                                            start=(j == 0), stop=(j == NB - 1 and p < 2))
                                last.then_inc(g_tile_mm, 1)
                                if i == 1 and not (first and par == 0 and p == 0):
                                    project(t - 1, 1 - par, p - 1 if first and par == 0 else p, first and p == 0)
                            if p == 2:
                                pe.wait_ge(g_own_ready, c + 1)
                                for b in range(CB):
                                    o = par * CW + b * D
                                    last = nc.tensor.matmul(hi_ps[par][:, b * P:(b + 1) * P], own[:, o:o + D], ident[:, :],
                                                            start=False, stop=(b == CB - 1))
                                last.then_inc(G.neigh_done, 1)
                    chunks(pe, body)
                project(3 * NC - 1, 1, 2, False)

            branch(pe, fast, general)

        @block.scalar
        def _(act):
            def h_relu(u):
                act.wait_ge(S.ln_ready, u + 1)
                relu_blocks(act, u, UB, lambda j: node_b[:, j * D:(j + 1) * D]).then_inc(hy_ready, 1)

            def a_sum(t, par, first):
                act.wait_ge(unit_mm, (t + 1) * UC)
                if not first:
                    act.wait_ge(S.nT_ready, t)
                nc.scalar.mul(lo_sum[:, :], lo_ps[par][:, :], 1 / (ONE * H_SCALE * LO)).then_inc(lo_ready, 1)

            def a_sig(t):
                act.wait_ge(S.zb_ready, t + 1)
                nc.scalar.activation(sig[:, :], zb[:, :], ACT.Sigmoid).then_inc(S.sig_ready, 1)

            def first_pass(turn, first):
                for par in range(2):
                    c = turn * 2 + par
                    if first and par == 0:
                        h_relu(0)
                    for u in range(UC):
                        if first and par == 0 and u + 1 < UC:
                            h_relu(u + 1)
                        for i in (2 * u, 2 * u + 1):
                            act.wait_ge(tile_in[i % RING], 16 * (c * (TC // RING) + i // RING + 1))
                            if not (first and par == 0 and i < 2):
                                act.wait_ge(counted, c * TC + i - 1)
                            nc.scalar.activation(unused[:, (i % 2) * TB * CW:(i % 2 + 1) * TB * CW], slot(i).bitcast(U32), ACT.Sign,
                                                 accum_out=nz_count[:, bass.ds(c * TC + i, 1)]).then_inc(counted, 1)
                        if first and par == 0:
                            act.wait_ge(hrest_ready, u + 1)
                            s = slice(u * UB * D, (u + 1) * UB * D)
                            nc.scalar.mul(node_a16[:, NB * D + u * UB * D:NB * D + (u + 1) * UB * D], node_b[:, s], LO).then_inc(S.h_ready, 1)
                        elif u == 1:
                            a_sum(c - 1, 1 - par, first)
                        elif u == 3:
                            a_sig(c - 1)
                        elif u == 4:
                            high_part(act, c - 1, c - 1, node_b16)
                        elif u == 5:
                            low_part(act, S, c - 1, c - 1, node_b16)
            chunks(act, first_pass)
            a_sum(NC - 1, 1, False)

            def fast():
                a_sig(NC - 1)
                high_part(act, NC - 1, NC - 1, node_b16)
                low_part(act, S, NC - 1, NC - 1, node_b16)
                for p in (1, 2):
                    chunks(act, lambda turn, first: [finish_act(act, S, turn, par, p, first, True) for par in range(2)])
                store_end(act, S)

            def general():
                for q in range(4):
                    act.wait_ge(G.ln_ready, q + 1)
                    relu_blocks(act, q, 16, lambda j: node_a[:, j * D:(j + 1) * D]).then_inc(G.h_ready, 1)
                for p in range(3):
                    chunks(act, lambda turn, first: [finish_act(act, G, turn, par, p, first, False) for par in range(2)])
                store_end(act, G)

            branch(act, fast, general)

        @block.vector
        def _(dve):
            nc.vector.memset(ones[:, :], 1.0).then_inc(ones_set, 1)
            nc.vector.memset(half16[:, :], 1 / ONE).then_inc(ones_set, 1)
            nc.vector.memset(first_row[:, :], 0.0).then_inc(row_zero, 1)
            dve.wait_ge(row_zero, 1)
            nc.vector.memset(first_row[0:1, :], 1.0).then_inc(ones_set, 1)
            dve.wait_ge(w_in, 64)
            nc.vector.tensor_tensor(wsq, w_sb[:, 0:D], w_sb[:, 0:D], ALU.mult).then_inc(wsq_ready, 1)

            def feature_scales():
                link = chain(dve, bound_step, 0)
                dve.wait_ge(wsum_done, 1)
                link(nc.vector.tensor_scalar(wsq, z_ps[:, 0:D], 1e-30, None, ALU.add))
                rsqrt(nc, link, wsq, bound, wtmp)
                link(nc.vector.tensor_tensor(bound, bound, wsq, ALU.mult))
                link(nc.vector.scalar_tensor_tensor(wtmp, b_sb[:, 0:D], -1.0, b_sb[:, 0:D], ALU.mult, ALU.max))
                link(nc.vector.scalar_tensor_tensor(bound, bound, SUM_BOUND, wtmp, ALU.mult, ALU.add))
                link(nc.vector.tensor_scalar(bound, bound, 1e-18, None, ALU.max))
                link(nc.vector.tensor_scalar(bound.bitcast(I32), bound.bitcast(I32), 0x7F800000, None, ALU.bitwise_and))
                nc.vector.tensor_scalar(s_row[:, :].bitcast(I32), bound.bitcast(I32), -1.0, float((127 + 127 + 14) << 23),
                                        ALU.mult, ALU.add).then_inc(s_ready, 1)
                link = chain(dve, alpha_step, 0)
                dve.wait_ge(s_col_done, 1)
                link(nc.vector.tensor_copy(alpha1[:, 0:1], misc_ps[:, 0:1]))
                link(nc.vector.tensor_scalar(alpha1[:, 0:1].bitcast(I32), alpha1[:, 0:1].bitcast(I32), -1.0, float((127 + 127 - 1) << 23),
                                             ALU.mult, ALU.add))
                link(nc.vector.tensor_scalar(alpha1[:, 1:2], alpha1[:, 0:1], 1 / LO, None, ALU.mult))

            def v_sum(t, par, first):
                dve.wait_ge(lo_ready, t + 1)
                nc.vector.scalar_tensor_tensor(half(nT, par), hi_ps[par][:, :], 1 / (ONE * H_SCALE), lo_sum[:, :],
                                               ALU.mult, ALU.add).then_inc(S.nT_ready, 1)
                if not first:
                    dve.wait_ge(S.dcol_done, t)
                nc.vector.tensor_scalar(deg_sb[:, :], deg_ps[par][:, :], 1.0, None, ALU.mult, ALU.add,
                                        accum_out=one_count[:, bass.ds(t, 1)]).then_inc(deg_sb_ready, 1)

            def v_bias(t):
                dve.wait_ge(S.z_done, t + 1)
                nc.vector.tensor_tensor(b3(zb[:, :]), b3(z_ps[:, :]), bias(0), ALU.add).then_inc(S.zb_ready, 1)
                dve.wait_ge(S.dcol_done, t + 1)
                nc.vector.tensor_scalar(deg[:, bass.ds(t * CB, CB)], misc_ps[:, 0:CB], 1.0, None, ALU.add).then_inc(S.deg_done, 1)
                dve.wait_ge(S.zb_ready, t + 1)
                s4 = s_row[:, :].unsqueeze(1).to_broadcast([P, CB, D])
                nc.vector.tensor_tensor(b3(y[:, :]), b3(zb[:, :]), s4, ALU.mult).then_inc(ys_ready, 1)

            def v_gate(t):
                dve.wait_ge(S.sig_ready, t + 1)
                dve.wait_ge(ys_ready, t + 1)
                nc.vector.tensor_tensor(y[:, :], y[:, :], sig[:, :], ALU.mult).then_inc(y_ready, 1)

            def h_high(u):
                dve.wait_ge(hy_ready, u + 1)
                s = slice(u * UB * D, (u + 1) * UB * D)
                nc.vector.tensor_copy(node_a16[:, s], node_b[:, s]).then_inc(hhi_ready, 1)

            def first_pass(turn, first):
                for par in range(2):
                    c = turn * 2 + par
                    if first and par == 0:
                        first_norm(dve, S, x_in[0], 0, UB, H_SCALE)
                    for u in range(UC):
                        if first and par == 0:
                            if u + 1 < UC:
                                first_norm(dve, S, x_in[u + 1], u + 1, UB, H_SCALE)
                            h_high(u)
                        g = c * UC + u
                        if not (first and par == 0 and u < 2):
                            dve.wait_ge(unit_mm, g - 1)
                        m = marks[:, (u % 2) * UB * CW:(u % 2 + 1) * UB * CW]
                        for i in range(2):
                            dve.wait_ge(tile_in[(2 * u + i) % RING], 16 * (c * (TC // RING) + (2 * u + i) // RING + 1))
                            nc.vector.tensor_scalar(m[:, i * TB * CW:(i + 1) * TB * CW], slot(2 * u + i), 1.0, float(ONE_BYTE),
                                                    ALU.is_equal, ALU.mult).then_inc(marked, 1)
                        m32 = m.bitcast(U32)
                        dve.wait_ge(marked, 2 * g + 2)
                        nc.vector.scalar_tensor_tensor(pack4, m32[:, 0:4 * WORDS], 1, m32[:, 4 * WORDS:8 * WORDS],
                                                       ALU.logical_shift_left, ALU.bitwise_or).then_inc(pack4_ready, 1)
                        dve.wait_ge(pack4_ready, g + 1)
                        nc.vector.scalar_tensor_tensor(pack2, pack4[:, 0:2 * WORDS], 2, pack4[:, 2 * WORDS:4 * WORDS],
                                                       ALU.logical_shift_right, ALU.bitwise_or).then_inc(pack2_ready, 1)
                        dve.wait_ge(pack2_ready, g + 1)
                        nc.vector.scalar_tensor_tensor(bits[:, bass.ds(g * WORDS, WORDS)], pack2[:, 0:WORDS], 4, pack2[:, WORDS:2 * WORDS],
                                                       ALU.logical_shift_right, ALU.bitwise_or).then_inc(bits_ready, 1)
                        if first and par == 0:
                            pass
                        elif u == 1:
                            v_sum(c - 1, 1 - par, first)
                        elif u == 3:
                            v_bias(c - 1)
                        elif u == 4:
                            v_gate(c - 1)
                        elif u == 5:
                            take_rest(dve, c - 1, c - 1, node_b16, first)
                    if first and par == 0:
                        feature_scales()
            chunks(dve, first_pass)
            v_sum(NC - 1, 1, False)

            dve.wait_ge(counted, NC * TC)
            nc.vector.tensor_reduce(nz_chunk[:, :], nz_count[:, :].rearrange("p (c i) -> p c i", i=TC), AX.X, ALU.add).then_inc(nz_ready, 1)
            link = chain(dve, flag_step, 0)
            dve.wait_ge(nz_total, 1)
            dve.wait_ge(deg_sb_ready, NC)
            link(nc.vector.tensor_tensor(differ[:, :], misc_ps[:, 0:NC], one_count[:, :], ALU.not_equal))
            link(nc.vector.tensor_reduce(flag_f[:, :], differ[:, :], AX.X, ALU.max))
            nc.vector.tensor_copy(flag[:, :], flag_f[:, :]).then_inc(flag_ready, 1)

            def fast():
                def unpack(c, v, start=False):
                    for gq in range(GC):
                        if not start:
                            dve.wait_ge(slot_used, (v - 1) * GC + gq + 1)
                        src = bits[:, bass.ds((c * GC + gq) * GB * WORDS, GB * WORDS)].rearrange("p (g w) -> p g w", g=GB)
                        dst = slot(gq).bitcast(U32).rearrange("p (g k w) -> p g k w", g=GB, k=UB)
                        for k in range(UB):
                            b = BIT[k]
                            shift = ALU.logical_shift_left if b < 6 else ALU.logical_shift_right
                            last = nc.vector.tensor_scalar(dst[:, :, k, :], src, abs(6 - b), ONE_WORD, shift, ALU.bitwise_and)
                        last.then_inc(unpacked, 1)

                dve.wait_ge(bits_ready, NC * UC)
                unpack(0, 0, True)
                v_bias(NC - 1)
                v_gate(NC - 1)
                take_rest(dve, NC - 1, NC - 1, node_b16)
                dve.wait_ge(S.deg_done, NC)
                rsqrt(nc, chain(dve, S.dinv_step, 0), deg[:, :], dinv[:, :], tmp[:, :])
                for p in (1, 2):
                    def body(turn, first):
                        for par in range(2):
                            c = turn * 2 + par
                            last = isinstance(turn, int) and turn > 0 and par == 1
                            if not (last and p == 2):
                                unpack(0 if last else c + 1, c + NC * (p - 1) + 1)
                            finish_dve(dve, S, turn, par, p, first, True)
                    chunks(dve, body, peel_last=True)

            def general():
                for q in range(4):
                    first_norm(dve, G, g_x_in[q], q, 16, 1.0)
                for p in range(3):
                    def body(turn, first):
                        for par in range(2):
                            c = turn * 2 + par
                            if p == 0:
                                acc = half(degacc, par)
                                for i in range(TC):
                                    g = c * TC + i
                                    dve.wait_ge(g_tile_in[i % RING], 16 * (c * (TC // RING) + i // RING + 1))
                                    if i == 0 and not first:
                                        dve.wait_ge(G.dcol_done, c - 1)
                                    til = slot(i).rearrange("p (q n) -> p n q", q=TB)
                                    nc.vector.tensor_reduce(acc if i == 0 else degtile, til, AX.X, ALU.add).then_inc(g_tile_red, 1)
                                    dve.wait_ge(g_tile_red, g + 1)
                                    if i > 0:
                                        last = nc.vector.tensor_tensor(acc, acc, degtile, ALU.add)
                                        last.then_inc(g_degacc_done if i == TC - 1 else g_degstep, 1)
                                        if i < TC - 1:
                                            dve.wait_ge(g_degstep, c * (TC - 2) + i)
                                dve.wait_ge(G.z_done, c + 1)
                                nc.vector.tensor_tensor(b3(zb[:, :]), b3(z_ps[:, :]), bias(0), ALU.add).then_inc(G.zb_ready, 1)
                                dve.wait_ge(G.dcol_done, c + 1)
                                nc.vector.tensor_scalar(deg[:, bass.ds(c * CB, CB)], misc_ps[:, 0:CB], 1.0, None, ALU.add).then_inc(G.deg_done, 1)
                                dve.wait_ge(G.sig_ready, c + 1)
                                nc.vector.tensor_tensor(blocks(node_b, c * CB, CB), zb[:, :], sig[:, :], ALU.mult).then_inc(G.node_ready, 1)
                            else:
                                finish_dve(dve, G, turn, par, p, first, False)
                    chunks(dve, body)
                    if p == 0:
                        dve.wait_ge(G.deg_done, NC)
                        link = chain(dve, G.dinv_step, 0)
                        rsqrt(nc, link, deg[:, :], dinv[:, :], tmp[:, :])
                        link(nc.vector.tensor_tensor(dinv[:, :], dinv[:, :], deg[:, :], ALU.mult))
                        link(nc.vector.reciprocal(dinv[:, :], dinv[:, :]))
                        link(nc.vector.tensor_scalar(tmp[:, :], deg[:, :], 0.0, HUGE, ALU.is_lt, ALU.mult))
                        link(nc.vector.tensor_scalar(tmp[:, :], tmp[:, :], HUGE, None, ALU.mult))
                        link(nc.vector.tensor_tensor(tmp[:, :], tmp[:, :], tmp[:, :], ALU.subtract))
                        link(nc.vector.tensor_tensor(dinv[:, :], dinv[:, :], tmp[:, :], ALU.add))

            branch(dve, fast, general)


def kernel(x, adj, L0_gnn_W, L0_gnn_b, L1_gnn_W, L1_gnn_b):
    import concourse.bacc as bacc
    from concourse.bass_utils import run_bass_kernel_spmd

    nc = bacc.Bacc("TRN2", target_bir_lowering=False, num_devices=1)
    tiles = np.asarray(adj).reshape(NC, CW, TC, TB, P).transpose(0, 2, 4, 3, 1)
    arrays = {
        "x": np.ascontiguousarray(x),
        "adj": np.ascontiguousarray(tiles).reshape(NC * TC * P, TB * CW),
        "w0": np.ascontiguousarray(L0_gnn_W),
        "b0": np.ascontiguousarray(L0_gnn_b).reshape(1, D),
        "w1t": np.ascontiguousarray(np.asarray(L1_gnn_W).T),
        "b1": np.ascontiguousarray(L1_gnn_b).reshape(1, D),
    }
    args = [nc.dram_tensor(k, a.shape, mybir.dt.from_np(a.dtype), kind="ExternalInput").ap() for k, a in arrays.items()]
    out = nc.dram_tensor("out", (N, D), F32, kind="ExternalOutput").ap()
    program(nc, *args, out)
    r = run_bass_kernel_spmd(nc, [arrays], core_ids=[0])
    return r.results[0]["out"]
```

```python
import numpy as np
import concourse.bass as bass
from concourse import mybir
from contextlib import ExitStack

F32 = mybir.dt.float32
I32 = mybir.dt.int32
ALU = mybir.AluOpType
ACT = mybir.ActivationFunctionType
AX = mybir.AxisListType

P = 128
N = 8192
D = 128
NB = N // P
CW = 512
CB = CW // P
NC = N // CW
TB = 4
TC = NB // TB
RING = 4
EPS = 1e-5
RSQRT_STEPS = 14
SCALE_STEPS = 5 + RSQRT_STEPS
MAGIC = float(0x5F3759DF)
HUGE = 3e38
F16 = mybir.dt.float16
F8 = mybir.dt.float8e4
U8 = mybir.dt.uint8
U32 = mybir.dt.uint32
U16 = mybir.dt.uint16
UB = 2 * TB
UC = NB // UB
WORDS = CW // 4
GB = 2
GC = UC // GB
H_SCALE = 1024.0
LO = 2048.0
ONE = 2.0
ONE_BYTE = 0x40
ONE_WORD = 0x40404040
BIT = {0: 1, 4: 0, 2: 3, 6: 2, 1: 5, 5: 4, 3: 7, 7: 6}
PARTS = [8, 8, 16, 16, 16]
PART_OF = [0, 1, 2, 2, 3, 3, 4, 4]
FIRST_JOB_TURN = 3
HAD = NC - 1
EARLY = UC
JOB_UNITS = UC // 2
PARTIALS = 2 * EARLY + HAD - EARLY
TURN_PAIRS = 6
AFTER = (0, 3, 5, 8, 11, 13)
LAST_AFTER = (0, 3, 5, 8, 11, 15)
JOIN_LATER = 2
NORM_PARTS = [8, 8, 16, 32]
NORM_AT = {0: 1, 1: 2, 2: 3}
H_RELU_AT = {1: 1, 2: 2, 4: 3, 6: 4}
SCALES_AT = 5
COUNT_STEPS = 22
SUM_BOUND = 93000.0


def chain(dve, step, start):
    count = [start]

    def link(ins):
        ins.then_inc(step, 1)
        count[0] = count[0] + 1
        dve.wait_ge(step, count[0])
    return link


def rsqrt(nc, link, v, r, a):
    link(nc.vector.tensor_scalar(r.bitcast(I32), v.bitcast(I32), 1, None, ALU.logical_shift_right))
    link(nc.vector.tensor_scalar(r.bitcast(I32), r.bitcast(I32), -1.0, MAGIC, ALU.mult, ALU.add))
    for _ in range(3):
        link(nc.vector.tensor_tensor(a, r, r, ALU.mult))
        link(nc.vector.tensor_tensor(a, a, v, ALU.mult))
        link(nc.vector.tensor_scalar(a, a, -0.5, 1.5, ALU.mult, ALU.add))
        link(nc.vector.tensor_tensor(r, r, a, ALU.mult))


def norm_scales(nc, link, stats, total, var, rstd, tmp):
    st = stats.rearrange("p (j s) -> p j s", s=6)
    tot = total.rearrange("p (j s) -> p j s", s=2)
    link(nc.vector.tensor_tensor(tot, st[:, :, 1:3], st[:, :, 4:6], ALU.add))
    link(nc.vector.tensor_tensor(tmp, st[:, :, 1], st[:, :, 4], ALU.subtract))
    link(nc.vector.scalar_tensor_tensor(tmp, tmp, 0.25, tmp, ALU.mult, ALU.mult))
    link(nc.vector.scalar_tensor_tensor(var, tot[:, :, 1], 1.0 / D, tmp, ALU.mult, ALU.add))
    link(nc.vector.tensor_scalar(var, var, EPS, None, ALU.add))
    rsqrt(nc, link, var, rstd, tmp)


class Turn:

    def __init__(self, turn, least):
        def low(n):
            return n, range(JOB_UNITS // 2), 2 * n

        def high(n):
            return n, range(JOB_UNITS // 2, JOB_UNITS), 2 * n + 1

        def whole(n):
            return n, range(JOB_UNITS), n + EARLY

        a = turn * 2
        self.jobs, self.before = {
            3: ([low(n) for n in range(6)], 0),
            4: ([low(6), low(7)] + [high(n) for n in range(4)], 6),
            5: ([whole(a - 2), whole(a - 1), high(a - 6), high(a - 5)], 12 + 4 * (turn - 5)),
            7: ([whole(12), whole(13), whole(14)], 20),
        }[least]
        self.first = least == FIRST_JOB_TURN
        self.pairs_before = TURN_PAIRS * (turn - FIRST_JOB_TURN)
        self.pairs = [(k, i) for k, job in enumerate(self.jobs) for i in range(len(job[1]) // 2)]
        after = LAST_AFTER if least == NC // 2 - 1 else AFTER
        self.low_at = {after[m] + JOIN_LATER: k for m, (k, i) in enumerate(self.pairs) if i == len(self.jobs[k][1]) // 2 - 1}
        self.pair_at = {after[m]: m for m in range(TURN_PAIRS)}


last_turn = Turn(NC // 2 - 1, NC // 2 - 1)
FIRST = (1, 3, 4, 5, 7)


class Signals:

    def __init__(self, sem, path):
        self.nT_ready = sem(path + "nT_ready")
        self.z_done = sem(path + "z_done")
        self.zb_ready = sem(path + "zb_ready")
        self.sig_ready = sem(path + "sig_ready")
        self.node_ready = sem(path + "node_ready")
        self.gated = sem(path + "gated")
        self.xch_in = [sem(path + "xch_in0"), sem(path + "xch_in1")]
        self.xn_ready = sem(path + "xn_ready")
        self.xn_out = [sem(path + "xn_out0"), sem(path + "xn_out1")]
        self.stat_done = sem(path + "stat_done")
        self.scale_step = sem(path + "scale_step")
        self.rs_done = sem(path + "rs_done")
        self.stats_ready = sem(path + "stats_ready")
        self.xb_ready = sem(path + "xb_ready")
        self.out_ready = sem(path + "out_ready")
        self.out_done = [sem(path + "out_done0"), sem(path + "out_done1")]
        self.neigh_done = sem(path + "neigh_done")
        self.ln_stat = sem(path + "ln_stat")
        self.ln_step = sem(path + "ln_step")
        self.ln_ready = sem(path + "ln_ready")
        self.h_ready = sem(path + "h_ready")
        self.deg_done = sem(path + "deg_done")
        self.dcol_done = sem(path + "dcol_done")
        self.dinv_step = sem(path + "dinv_step")


def program(nc, x, adj, w0, b0, w1t, b1, out):
    adj_t = adj.rearrange("(t p) n -> t p n", p=P)
    x_v = x.rearrange("(j p) d -> p j d", p=P)
    out_v = out.rearrange("(j p) d -> p j d", p=P)
    ctx = ExitStack()
    with ctx:
        def sb(name, shape, dt=F32):
            return ctx.enter_context(nc.sbuf_tensor(name, shape, dt))

        def pb(name):
            return ctx.enter_context(nc.psum_tensor(name, [P, CW], F32))

        def sem(name):
            return ctx.enter_context(nc.semaphore(name))

        xn_dram = nc.dram_tensor("xn_scratch", [N, D], F32, kind="Internal").ap()
        part_dram = nc.dram_tensor("part_scratch", [PARTIALS * P, CW], F32, kind="Internal").ap()
        part_v = part_dram.rearrange("(c p) n -> p c n", p=P)
        xn_v = xn_dram.rearrange("(j p) d -> p j d", p=P)

        node_a = sb("node_a", [P, NB * D])
        node_b = sb("node_b", [P, NB * D])
        ring = sb("ring", [P, RING * TB * CW])
        bits = sb("bits", [P, NC * UC * WORDS], U32)
        marks = sb("marks", [P, 2 * UB * CW], U8)
        unused = sb("unused", [P, TB * CW], U8)
        w_sb = sb("w_sb", [P, 2 * D])
        b_sb = sb("b_sb", [P, 2 * D])
        ident = sb("ident", [P, P])
        ident16 = sb("ident16", [P, P], F16)
        ones = sb("ones", [P, P])
        ones16 = sb("ones16", [P, 1], F16)
        job_slot = sb("job_slot", [P, 2 * UB * CW], U8)
        count16 = sb("count16", [P, CW], F16)
        first_row = sb("first_row", [P, 1])
        stats = sb("stats", [P, NB * 6])
        mv = sb("mv", [P, NB * 2])
        var = sb("var", [P, NB])
        rstd = sb("rstd", [P, NB])
        tmp = sb("tmp", [P, NB])
        nmr = sb("nmr", [P, NB])
        deg = sb("deg", [P, NB])
        dinv = sb("dinv", [P, NB])
        nz_count = sb("nz_count", [P, NC * TC])
        nz_chunk = sb("nz_chunk", [P, NC])
        one_count = sb("one_count", [P, NC])
        differ = sb("differ", [P, NC])
        flag_f = sb("flag_f", [P, 1])
        flag = sb("flag", [P, 1], I32)
        s_row = sb("s_row", [P, D])
        alpha1 = sb("alpha1", [P, 2])
        nT = sb("nT", [P, 2 * CW])
        lo_sum = sb("lo_sum", [P, CW])
        zb = sb("zb", [P, CW])
        sig = sb("sig", [P, CW])
        y = sb("y", [P, CW])
        xch = sb("xch", [P, 2 * CW])
        xnew = sb("xnew", [P, 2 * CW])
        pack4, pack2 = xnew[:, 0:4 * WORDS].bitcast(U32), xch[:, 0:2 * WORDS].bitcast(U32)
        count8 = xch[:, 2 * WORDS:3 * WORDS].bitcast(U32)
        count_a = xch[:, CW:2 * CW].bitcast(U32)
        job_sum = xnew[:, CW:2 * CW]
        wsq, bound, wtmp = xch[:, 3 * WORDS:3 * WORDS + D], xnew[:, CW:CW + D], xnew[:, CW + D:CW + 2 * D]
        scratch = marks[:, :].bitcast(F32)
        degacc, own = scratch[:, 0:2 * CW], scratch[:, 2 * CW:4 * CW]
        degtile = xch[:, CW:2 * CW]

        hi_ps = [pb("hi0_ps"), pb("hi1_ps")]
        lo_ps = [pb("lo0_ps"), pb("lo1_ps")]
        job_hi_ps, job_lo_ps = pb("job_hi_ps"), pb("job_lo_ps")
        z_ps = pb("z_ps")
        misc_ps = pb("misc_ps")

        S = Signals(sem, "")
        G = Signals(sem, "g_")
        x_in = [sem(f"x_in{u}") for u in range(len(NORM_PARTS))]
        w_in = sem("w_in")
        tile_in = [sem(f"tile_in{s}") for s in range(RING)]
        ones_set, ident_zero, ident_set, ident16_set = sem("ones_set"), sem("ident_zero"), sem("ident_set"), sem("ident16_set")
        row_zero = sem("row_zero")
        hy_ready, hhi_ready, hrest_ready = sem("hy_ready"), sem("hhi_ready"), sem("hrest_ready")
        count_step, counted16 = sem("count_step"), sem("counted16")
        job_unpacked, job_used, job_lo_ready, job_sum_ready, part_out = (
            sem("job_unpacked"), sem("job_used"), sem("job_lo_ready"), sem("job_sum_ready"), sem("part_out"))
        part_whole = sem("part_whole")
        part_arrived, joined = [sem("part_arrived0"), sem("part_arrived1")], sem("joined")
        marked, counted, unit_mm = sem("marked"), sem("counted"), sem("unit_mm")
        pack4_ready, pack2_ready, bits_ready = sem("pack4_ready"), sem("pack2_ready"), sem("bits_ready")
        lo_ready = sem("lo_ready")
        ys_ready, y_ready, hi_ready, rest_ready = sem("ys_ready"), sem("y_ready"), sem("hi_ready"), sem("rest_ready")
        wsq_ready, wsum_done, bound_step, s_ready, s_col_done, alpha_step = (
            sem("wsq_ready"), sem("wsum_done"), sem("bound_step"), sem("s_ready"), sem("s_col_done"), sem("alpha_step"))
        flag_step, differ_ready, differ_sum, flag_ready = sem("flag_step"), sem("differ_ready"), sem("differ_sum"), sem("flag_ready")
        settled = sem("settled")
        unpacked, slot_used = sem("unpacked"), sem("slot_used")
        g_x_in = [sem(f"g_x_in{q}") for q in range(4)]
        g_tile_in = [sem(f"g_tile_in{s}") for s in range(RING)]
        g_tile_mm, g_tile_red, g_degstep, g_degacc_done, g_own_ready, g_dinv_done = (
            sem("g_tile_mm"), sem("g_tile_red"), sem("g_degstep"), sem("g_degacc_done"), sem("g_own_ready"), sem("g_dinv_done"))

        node_a16, node_b16 = node_a[:, :].bitcast(F16), node_b[:, :].bitcast(F16)

        def blocks(buf, first, n):
            return buf[:, bass.ds(first * D, n * D)]

        def lo_blocks(buf, first, n):
            return buf[:, bass.ds(first * D + NB * D, n * D)]

        def b3(ap):
            return ap.rearrange("p (j d) -> p j d", d=D)

        def bias(which):
            return b_sb[:, which * D:(which + 1) * D].unsqueeze(1).to_broadcast([P, CB, D])

        def half(buf, par):
            return buf[:, par * CW:(par + 1) * CW]

        def slot(i):
            return ring[:, (i % RING) * TB * CW:(i % RING + 1) * TB * CW]

        def chunks(eng, body, cuts=(1,), peel_last=False):
            body(0, 0)
            for a, b in zip(cuts, [*cuts[1:], NC // 2 - peel_last]):
                if b == a + 1:
                    body(a, a)
                elif b > a:
                    with eng.Fori(a, b) as turn:
                        body(turn, a)
            if peel_last:
                body(NC // 2 - 1, NC // 2 - 1)

        SECOND = (1, EARLY // 2, NC // 2 - 2, NC // 2 - 1)

        def jobs_had(p, least, par):
            c = 2 * least + par
            return (c < HAD) + (c < EARLY) if p == 1 else 0

        def slots(had, par):
            start = par * GC // 2 if had else HAD * GC // 2
            groups = range(GC // 2, GC) if had else range(GC)
            return [(gq, (start + k) % RING) for k, gq in enumerate(groups)]

        def first_slot(v, later):
            return v * GC - HAD * GC // 2 if later else v * (GC // 2)

        def part_in(par, k):
            return scratch[:, (2 * par + k) * CW:(2 * par + k + 1) * CW]

        def unpack_bit(dst, src, k):
            shift = ALU.logical_shift_left if BIT[k] < 6 else ALU.logical_shift_right
            return nc.vector.tensor_scalar(dst, src, abs(6 - BIT[k]), ONE_WORD, shift, ALU.bitwise_and)

        def branch(eng, fast, general):
            eng.wait_ge(flag_ready, 1)
            found = eng.value_load(flag[0:1, 0:1], min_val=0, max_val=1)
            with eng.If(found == 0):
                fast()
            with eng.Else():
                general()


        def load_chunk(eng, S, turn, par, p, first):
            c = turn * 2 + par
            if p == 1 and not first:
                eng.wait_ge(S.xn_ready, c - 1)
            if p == 2 and first:
                eng.wait_ge(S.xn_ready, NC - 1 + par)
            if p == 2 and not first:
                eng.wait_ge(S.xb_ready, c - 1)
            if p == 2 and first and par == 0:
                eng.wait_ge(S.xn_out[0], 16 * NC // 2)
                eng.wait_ge(S.xn_out[1], 16 * NC // 2)
            src = x_v if p == 1 else xn_v
            eng.dma_start(b3(half(xch, par)), src[:, bass.ds(c * CB, CB), :]).then_inc(S.xch_in[par], 16)

        def project_z(pe, S, t, par, p, first):
            pe.wait_ge(S.nT_ready, t + 1)
            if not first:
                pe.wait_ge(S.zb_ready, t)
            w = w_sb[:, 0:D] if p < 2 else w_sb[:, D:2 * D]
            for b in range(CB):
                last = nc.tensor.matmul(z_ps[:, b * D:(b + 1) * D], nT[:, par * CW + b * P:par * CW + (b + 1) * P], w,
                                        start=True, stop=True)
            last.then_inc(S.z_done, 1)

        def first_norm(dve, S, arrived, part, a, n, scale):
            s = slice(a, a + n)
            dve.wait_ge(arrived, 16)
            for j in range(a, a + n):
                last = nc.vector.bn_stats(stats[:, j * 6:j * 6 + 6], node_b[:, j * D:(j + 1) * D])
            last.then_inc(S.ln_stat, 1)
            dve.wait_ge(S.ln_stat, part + 1)
            link = chain(dve, S.ln_step, (SCALE_STEPS + 1) * part)
            norm_scales(nc, link, stats[:, a * 6:(a + n) * 6], mv[:, a * 2:(a + n) * 2], var[:, s], rstd[:, s], tmp[:, s])
            link(nc.vector.tensor_scalar(rstd[:, s], rstd[:, s], scale, None, ALU.mult))
            twice_mean = mv[:, a * 2:(a + n) * 2].rearrange("p (j s) -> p j s", s=2)[:, :, 0]
            nc.vector.scalar_tensor_tensor(nmr[:, s], twice_mean, -0.5, rstd[:, s], ALU.mult, ALU.mult).then_inc(S.ln_ready, 1)

        def relu_blocks(act, a, n, out_of):
            for j in range(a, a + n):
                last = nc.scalar.activation(out_of(j), node_b[:, j * D:(j + 1) * D], ACT.Relu,
                                            bias=nmr[:, j:j + 1], scale=rstd[:, j:j + 1])
            return last

        def finish_dve(dve, S, turn, par, p, first, split, had=0, meanwhile=None):
            c = turn * 2 + par
            t = c + NC * p
            if split:
                dve.wait_ge(lo_ready, t + 1)
                both = lo_sum[:, :] if had else half(nT, par)
                nc.vector.scalar_tensor_tensor(both, hi_ps[par][:, :], alpha1[:, 0:1] if p == 1 else 1 / (ONE * H_SCALE),
                                               lo_sum[:, :], ALU.mult, ALU.add).then_inc(joined if had else S.nT_ready, 1)
                if had:
                    dve.wait_ge(joined, c + 1)
                    if had == 2:
                        dve.wait_ge(part_whole, c + 1)
                    else:
                        dve.wait_ge(part_arrived[par], 16 * turn + 16)
                    nc.vector.tensor_tensor(half(nT, par), lo_sum[:, :], part_in(par, 0), ALU.add).then_inc(S.nT_ready, 1)
            if meanwhile:
                meanwhile()
            zb3, z3, x_c, xn = b3(zb[:, :]), b3(z_ps[:, :]), half(xch, par), half(xnew, par)
            dve.wait_ge(S.z_done, t + 1)
            if p == 1:
                nc.vector.tensor_tensor(zb3, z3, bias(0), ALU.add).then_inc(S.zb_ready, 1)
                dve.wait_ge(S.sig_ready, t + 1)
                nc.vector.tensor_tensor(zb[:, :], zb[:, :], sig[:, :], ALU.mult).then_inc(S.gated, 1)
                dve.wait_ge(S.gated, c + 1)
                dve.wait_ge(S.xch_in[par], 16 * turn + 16)
                if not first:
                    dve.wait_ge(S.xn_out[par], 16 * turn)
                nc.vector.tensor_tensor(xn, x_c, zb[:, :], ALU.add).then_inc(S.xn_ready, 1)
                dve.wait_ge(S.xn_ready, c + 1)
                for b in range(CB):
                    last = nc.vector.bn_stats(stats[:, b * 6:b * 6 + 6], xn[:, b * D:(b + 1) * D])
                last.then_inc(S.stat_done, 1)
                dve.wait_ge(S.stat_done, c + 1)
                if not (first and par == 0):
                    dve.wait_ge(y_ready if split else S.node_ready, t)
                norm_scales(nc, chain(dve, S.scale_step, c * SCALE_STEPS), stats[:, 0:6 * CB], mv[:, 0:2 * CB],
                            var[:, 0:CB], rstd[:, 0:CB], tmp[:, 0:CB])
                nc.vector.scalar_tensor_tensor(rstd[:, 0:CB], rstd[:, 0:CB], H_SCALE if split else 1.0,
                                               dinv[:, bass.ds(c * CB, CB)], ALU.mult, ALU.mult).then_inc(S.rs_done, 1)
                dve.wait_ge(S.rs_done, c + 1)
                twice_mean = mv[:, 0:2 * CB].rearrange("p (j s) -> p j s", s=2)[:, :, 0]
                nc.vector.scalar_tensor_tensor(nmr[:, 0:CB], twice_mean, -0.5, rstd[:, 0:CB], ALU.mult, ALU.mult).then_inc(S.stats_ready, 1)
            if p == 2:
                dd = dinv[:, bass.ds(c * CB, CB)].unsqueeze(2).to_broadcast([P, CB, D])
                nc.vector.tensor_tensor(zb3, z3, dd, ALU.mult).then_inc(S.zb_ready, 1)
                dve.wait_ge(S.zb_ready, t + 1)
                dve.wait_ge(S.xch_in[par], 16 * (NC // 2 + turn + 1))
                if first:
                    dve.wait_ge(S.xn_out[par], 16 * (NC // 2))
                else:
                    dve.wait_ge(S.out_done[par], 16 * turn)
                nc.vector.tensor_tensor(b3(xn), b3(x_c), bias(1), ALU.add).then_inc(S.xb_ready, 1)
                dve.wait_ge(S.xb_ready, c + 1)
                nc.vector.tensor_tensor(xn, xn, zb[:, :], ALU.add).then_inc(S.out_ready, 1)

        def relu_of_norm(act, S, t, par, split):
            c = t - NC
            act.wait_ge(S.stats_ready, c + 1)
            if split:
                act.wait_ge(S.node_ready, t)
            for b in range(CB):
                to = y[:, b * D:(b + 1) * D] if split else blocks(node_a, c * CB + b, 1)
                last = nc.scalar.activation(to, xnew[:, par * CW + b * D:par * CW + (b + 1) * D],
                                            ACT.Relu, bias=nmr[:, b:b + 1], scale=rstd[:, b:b + 1])
            last.then_inc(y_ready if split else S.node_ready, 1)

        def store_xn(act, S, c, par):
            act.wait_ge(S.xn_ready, c + 1)
            act.dma_start(xn_v[:, bass.ds(c * CB, CB), :], b3(half(xnew, par))).then_inc(S.xn_out[par], 16)

        def finish_rows(act, S, t, c, par):
            high_part(act, t, c, node_a16)
            store_xn(act, S, c, par)
            low_part(act, S, t, c, node_a16)

        def finish_act(act, S, turn, par, p, first, split, had=0):
            c = turn * 2 + par
            t = c + NC * p
            if p > 0 and not split:
                load_chunk(act, S, turn, par, p, first)
            if p == 2:
                act.wait_ge(S.neigh_done, c + 1)
            elif split:
                act.wait_ge(slot_used, first_slot(c + 1, not had))
            else:
                act.wait_ge(g_tile_mm, TC * (t + 1))
            if split:
                act.wait_ge(S.nT_ready, t)
                scale = alpha1[:, 1:2] if p == 1 else 1 / (ONE * H_SCALE * LO)
                nc.scalar.activation(lo_sum[:, :], lo_ps[par][:, :], ACT.Identity, scale=scale).then_inc(lo_ready, 1)
            else:
                nc.scalar.copy(half(nT, par), hi_ps[par][:, :]).then_inc(S.nT_ready, 1)
            if p == 1 and split and not (first and par == 0):
                relu_of_norm(act, S, t - 1, 1 - par, split)
            if p < 2:
                act.wait_ge(S.zb_ready, t + 1)
                nc.scalar.activation(sig[:, :], zb[:, :], ACT.Sigmoid).then_inc(S.sig_ready, 1)
            if p == 1 and split:
                if not (first and par == 0):
                    finish_rows(act, S, t - 1, c - 1, 1 - par)
                if isinstance(turn, int) and turn == NC // 2 - 1 and par == 1:
                    relu_of_norm(act, S, t, par, split)
                    finish_rows(act, S, t, c, par)
            elif p == 1:
                relu_of_norm(act, S, t, par, split)
                store_xn(act, S, c, par)
            if p == 2:
                act.wait_ge(S.out_ready, c + 1)
                act.dma_start(out_v[:, bass.ds(c * CB, CB), :], b3(half(xnew, par))).then_inc(S.out_done[par], 16)

        def high_part(act, t, c, node):
            act.wait_ge(y_ready, t + 1)
            nc.scalar.copy(blocks(node, c * CB, CB), y[:, :]).then_inc(hi_ready, 1)

        def take_rest(pool, t, c, node):
            pool.wait_ge(hi_ready, t + 1)
            nc.gpsimd.tensor_tensor(y[:, :], y[:, :], blocks(node, c * CB, CB), ALU.subtract).then_inc(rest_ready, 1)

        def scale_and_gate(pool, t, first=False):
            pool.wait_ge(S.zb_ready, t + 1)
            if not first:
                pool.wait_ge(S.node_ready, t)
            s4 = s_row[:, :].unsqueeze(1).to_broadcast([P, CB, D])
            nc.gpsimd.tensor_tensor(b3(y[:, :]), b3(zb[:, :]), s4, ALU.mult).then_inc(ys_ready, 1)
            pool.wait_ge(S.sig_ready, t + 1)
            pool.wait_ge(ys_ready, t + 1)
            nc.gpsimd.tensor_tensor(y[:, :], y[:, :], sig[:, :], ALU.mult).then_inc(y_ready, 1)

        def low_part(act, S, t, c, node):
            act.wait_ge(rest_ready, t + 1)
            nc.scalar.mul(lo_blocks(node, c * CB, CB), y[:, :], LO).then_inc(S.node_ready, 1)

        def store_end(act, S):
            for par in range(2):
                act.wait_ge(S.out_done[par], 16 * NC // 2)

        block = ctx.enter_context(nc.Block())

        @block.sync
        def _(sp):
            def load_x(a, n, arrived):
                sp.dma_start(b3(node_b[:, a * D:(a + n) * D]), x_v[:, a:a + n, :]).then_inc(arrived, 16)

            load_x(0, NORM_PARTS[0], x_in[0])
            sp.dma_start(w_sb[:, 0:D], w0).then_inc(w_in, 16)
            sp.dma_start(w_sb[:, D:2 * D], w1t).then_inc(w_in, 16)
            sp.dma_start(b_sb[:, 0:D], b0.to_broadcast([P, D])).then_inc(w_in, 16)
            sp.dma_start(b_sb[:, D:2 * D], b1.to_broadcast([P, D])).then_inc(w_in, 16)

            def first_pass(turn, least):
                first = least == 0
                for par in range(2):
                    c = turn * 2 + par
                    for i in range(TC):
                        g = c * TC + i
                        if first and par == 0 and i % 2 == 0 and 0 < i // 2 < len(NORM_PARTS):
                            load_x(sum(NORM_PARTS[:i // 2]), NORM_PARTS[i // 2], x_in[i // 2])
                        if not (first and par == 0 and i < RING):
                            sp.wait_ge(marked, g - RING + 1)
                            sp.wait_ge(counted, g - RING + 1)
                        sp.dma_start(slot(i), adj_t[bass.ds(g, 1), :, :].rearrange("o p n -> p (o n)")).then_inc(tile_in[i % RING], 16)
            chunks(sp, first_pass)

            def fast():
                sp.wait_ge(part_out, 16 * PARTIALS)
                sp.wait_ge(unit_mm, NC * UC)
                for p in (1, 2):
                    def body(turn, least):
                        first = least == 0
                        for par in range(2):
                            load_chunk(sp, S, turn, par, p, first)
                            had = jobs_had(p, least, par)
                            if had:
                                c = turn * 2 + par
                                if not first:
                                    sp.wait_ge(S.nT_ready, NC + c - 1)
                                first_part = 2 * c if had == 2 else EARLY + c
                                sp.dma_start(scratch[:, 2 * par * CW:(2 * par + had) * CW].rearrange("p (k n) -> p k n", k=had),
                                             part_v[:, bass.ds(first_part, had), :]).then_inc(part_arrived[par], 16)
                    chunks(sp, body, SECOND if p == 1 else (1,))

            def general():
                for q in range(4):
                    load_x(q * 16, 16, g_x_in[q])
                for p in range(3):
                    def body(turn, least):
                        first = least == 0
                        for par in range(2):
                            c = turn * 2 + par
                            for i in range(TC):
                                g = c * TC + i + NC * TC * p
                                if not (p == 0 and first and par == 0 and i < RING):
                                    sp.wait_ge(g_tile_mm, g - RING + 1)
                                    if p == 0 or (p == 1 and first and par == 0 and i < RING):
                                        sp.wait_ge(g_tile_red, g - RING + 1)
                                sp.dma_start(slot(i), adj_t[bass.ds(c * TC + i, 1), :, :].rearrange("o p n -> p (o n)")
                                             ).then_inc(g_tile_in[i % RING], 16)
                    chunks(sp, body)

            branch(sp, fast, general)

        @block.gpsimd
        def _(pool):
            nc.gpsimd.memset(ident[:, :], 0.0).then_inc(ident_zero, 1)
            pool.wait_ge(ident_zero, 1)
            nc.gpsimd.affine_select(out=ident[:, :], in_=ident[:, :], compare_op=ALU.not_equal, fill=1.0, base=0,
                                    pattern=[[-1, P]], channel_multiplier=1).then_inc(ident_set, 1)
            pool.wait_ge(ident_set, 1)
            nc.gpsimd.tensor_scalar(ident16[:, :], ident[:, :], ONE, 0.0, ALU.mult, ALU.add).then_inc(ident16_set, 1)
            a = 0
            for part, n in enumerate(PARTS):
                pool.wait_ge(hy_ready, part + 1)
                s, low = slice(a * D, (a + n) * D), slice((NB + a) * D, (NB + a + n) * D)
                nc.gpsimd.tensor_scalar(node_a16[:, s], node_b[:, s], 1.0, 1.0, ALU.mult, ALU.mult).then_inc(hhi_ready, 1)
                pool.wait_ge(hhi_ready, part + 1)
                nc.gpsimd.tensor_tensor(node_b[:, s], node_b[:, s], node_a16[:, s], ALU.subtract).then_inc(hrest_ready, 1)
                pool.wait_ge(hrest_ready, part + 1)
                nc.gpsimd.tensor_scalar(node_a16[:, low], node_b[:, s], LO, 1.0, ALU.mult, ALU.mult).then_inc(S.h_ready, 1)
                a += n

            def first_pass(turn, least):
                for par in range(2):
                    c = turn * 2 + par
                    if not (least == 0 and par == 0):
                        scale_and_gate(pool, c - 1, least == 0 and par == 1)
                        take_rest(pool, c - 1, c - 1, node_b16)
            chunks(pool, first_pass)

            def fast():
                scale_and_gate(pool, NC - 1)
                take_rest(pool, NC - 1, NC - 1, node_b16)

                def add_partials(turn, par):
                    pool.wait_ge(part_arrived[par], 16 * turn + 16)
                    nc.gpsimd.tensor_tensor(part_in(par, 0), part_in(par, 0), part_in(par, 1), ALU.add).then_inc(part_whole, 1)

                add_partials(0, 0)

                def body(turn, least):
                    for par in range(2):
                        if jobs_had(1, least + par, 1 - par) == 2:
                            add_partials(turn + par, 1 - par)
                        take_rest(pool, turn * 2 + par + NC, turn * 2 + par, node_a16)
                chunks(pool, body, (1, EARLY // 2 - 1, EARLY // 2))

            def general():
                def body(turn, least):
                    for par in range(2):
                        c = turn * 2 + par
                        if least == 0:
                            pool.wait_ge(G.node_ready, 2 * NC)
                        else:
                            pool.wait_ge(G.neigh_done, c - 1)
                        nc.gpsimd.tensor_copy(half(own, par), blocks(node_a, c * CB, CB)).then_inc(g_own_ready, 1)
                chunks(pool, body)

            branch(pool, fast, general)

        @block.tensor
        def _(pe):
            pe.wait_ge(ones_set, 3)
            pe.wait_ge(ident_set, 1)
            pe.wait_ge(w_in, 64)

            def settle():
                pe.sem_inc(settled, 1)

            def project_first(t, par, first):
                project_z(pe, S, t, par, 0, first)
                pe.wait_ge(counted16, t + 1)
                if not first:
                    pe.wait_ge(S.deg_done, t)
                for b in range(CB):
                    last = nc.tensor.matmul(misc_ps[:, b:b + 1], count16[:, b * P:(b + 1) * P], ones16[:, :], start=True, stop=True)
                last.then_inc(S.dcol_done, 1)

            def job_pair(now, m, other_rows):
                k, i = now.pairs[m]
                units = now.jobs[k][1]
                if i == 0 and not (now.first and k == 0):
                    pe.wait_ge(job_sum_ready, now.before + k)
                pe.wait_ge(job_unpacked, now.pairs_before + m + 1)
                settle()
                for b in range(2 * UB):
                    j = units[2 * i] * UB + b
                    if other_rows and b == UB:
                        pe.wait_ge(S.node_ready, JOB_UNITS * UB // CB)
                    bytes_ = job_slot[:, b * CW:(b + 1) * CW].bitcast(F8)
                    ends = dict(start=(i == 0 and b == 0), stop=(2 * i + 2 == len(units) and b == 2 * UB - 1))
                    nc.tensor.matmul(job_hi_ps[:, :], node_b16[:, j * D:(j + 1) * D], bytes_, **ends)
                    last = nc.tensor.matmul(job_lo_ps[:, :], node_b16[:, (NB + j) * D:(NB + j + 1) * D], bytes_, **ends)
                last.then_inc(job_used, 1)

            pe.wait_ge(wsq_ready, 1)
            nc.tensor.matmul(z_ps[:, 0:D], ones[:, :], wsq, start=True, stop=True).then_inc(wsum_done, 1)

            def first_pass(turn, least):
                first = least == 0
                now = Turn(turn, least) if least >= FIRST_JOB_TURN else None
                if least == FIRST_JOB_TURN:
                    pe.wait_ge(S.node_ready, JOB_UNITS // 2 * UB // CB)
                for par in range(2):
                    c = turn * 2 + par
                    for u in range(UC):
                        if first and par == 0 and (u == 0 or PART_OF[u] > PART_OF[u - 1]):
                            pe.wait_ge(S.h_ready, PART_OF[u] + 1)
                        for i in range(UB):
                            j = u * UB + i
                            if i % TB == 0:
                                pe.wait_ge(marked, c * TC + 2 * u + i // TB + 1)
                                settle()
                            m = marks[:, ((u % 2) * UB + i) * CW:((u % 2) * UB + i + 1) * CW].bitcast(F8)
                            ends = dict(start=(j == 0), stop=(j == NB - 1))
                            nc.tensor.matmul(hi_ps[par][:, :], node_a16[:, j * D:(j + 1) * D], m, **ends)
                            last = nc.tensor.matmul(lo_ps[par][:, :], node_a16[:, (NB + j) * D:(NB + j + 1) * D], m, **ends)
                        last.then_inc(unit_mm, 1)
                        if first and par == 0 and u == SCALES_AT:
                            pe.wait_ge(s_ready, 1)
                            nc.tensor.matmul(misc_ps[:, 0:1], s_row[:, :], first_row[:, :], start=True, stop=True).then_inc(s_col_done, 1)
                            pe.wait_ge(alpha_step, 1)
                        if u == 1 and not (first and par == 0):
                            project_first(c - 1, 1 - par, first)
                        if now and par * UC + u in now.pair_at:
                            m = now.pair_at[par * UC + u]
                            job_pair(now, m, least == FIRST_JOB_TURN + 1 and now.pairs[m] == (2, 0))
            chunks(pe, first_pass, FIRST)
            pe.wait_ge(differ_ready, 1)
            nc.tensor.matmul(misc_ps[:, CB:CB + 1], ones[:, :], flag_f[:, :], start=True, stop=True).then_inc(differ_sum, 1)

            def fast():
                pe.wait_ge(ident16_set, 1)
                for p in (1, 2):
                    node = node_b16 if p == 1 else node_a16

                    def body(turn, least):
                        first = least == 0
                        for par in range(2):
                            c = turn * 2 + par
                            had = jobs_had(p, least, par)
                            v = first_slot(c + NC * (p - 1), not had)
                            for k, (gq, where) in enumerate(slots(had, par)):
                                pe.wait_ge(unpacked, v + k + 1)
                                settle()
                                for i in range(GB * UB):
                                    j = gq * GB * UB + i
                                    if first and par == 0 and j % CB == 0:
                                        pe.wait_ge(S.node_ready, NC * (p - 1) + j // CB + 1)
                                        settle()
                                    m = slot(where)[:, i * WORDS:(i + 1) * WORDS].bitcast(F8)
                                    ends = dict(start=(k == 0 and i == 0), stop=(j == NB - 1 and p == 1))
                                    nc.tensor.matmul(hi_ps[par][:, :], node[:, j * D:(j + 1) * D], m, **ends)
                                    last = nc.tensor.matmul(lo_ps[par][:, :], node[:, (NB + j) * D:(NB + j + 1) * D], m, **ends)
                                    if k == 0 and i == 5:
                                        if first and par == 0 and p == 1:
                                            project_first(NC - 1, 1, False)
                                        else:
                                            project_z(pe, S, c - 1 + NC * p, 1 - par, p - 1 if first and par == 0 else p, False)
                                last.then_inc(slot_used, 1)
                            if p == 2:
                                for b in range(CB):
                                    cols = slice(b * P, (b + 1) * P)
                                    nc.tensor.matmul(hi_ps[par][:, cols], blocks(node, c * CB + b, 1), ident16[:, :], start=False, stop=(b == CB - 1))
                                    last = nc.tensor.matmul(lo_ps[par][:, cols], lo_blocks(node, c * CB + b, 1), ident16[:, :],
                                                            start=False, stop=(b == CB - 1))
                                last.then_inc(S.neigh_done, 1)
                    chunks(pe, body, SECOND if p == 1 else (1,))
                project_z(pe, S, 3 * NC - 1, 1, 2, False)

            def general():
                def project(t, par, p, first):
                    project_z(pe, G, t, par, p, first)
                    if p == 0:
                        pe.wait_ge(g_degacc_done, t + 1)
                        if not first:
                            pe.wait_ge(G.deg_done, t)
                        for b in range(CB):
                            last = nc.tensor.matmul(misc_ps[:, b:b + 1], degacc[:, par * CW + b * P:par * CW + (b + 1) * P],
                                                    ones[:, 0:1], start=True, stop=True)
                        last.then_inc(G.dcol_done, 1)

                for p in range(3):
                    h = node_b if p == 1 else node_a

                    def body(turn, least):
                        first = least == 0
                        for par in range(2):
                            c = turn * 2 + par
                            t = c + NC * p
                            for i in range(TC):
                                pe.wait_ge(g_tile_in[i % RING], 16 * (t * (TC // RING) + i // RING + 1))
                                if p == 0 and first and par == 0 and i % 4 == 0:
                                    pe.wait_ge(G.h_ready, i // 4 + 1)
                                if p > 0 and first and par == 0:
                                    pe.wait_ge(G.node_ready, NC * (p - 1) + i + 1)
                                for q in range(TB):
                                    j = i * TB + q
                                    last = nc.tensor.matmul(hi_ps[par][:, :], h[:, j * D:(j + 1) * D], slot(i)[:, q * CW:(q + 1) * CW],
                                                            start=(j == 0), stop=(j == NB - 1 and p < 2))
                                last.then_inc(g_tile_mm, 1)
                                if i == 1 and not (first and par == 0 and p == 0):
                                    project(t - 1, 1 - par, p - 1 if first and par == 0 else p, first and p == 0)
                            if p == 2:
                                pe.wait_ge(g_own_ready, c + 1)
                                for b in range(CB):
                                    o = par * CW + b * D
                                    last = nc.tensor.matmul(hi_ps[par][:, b * P:(b + 1) * P], own[:, o:o + D], ident[:, :],
                                                            start=False, stop=(b == CB - 1))
                                last.then_inc(G.neigh_done, 1)
                    chunks(pe, body)
                project(3 * NC - 1, 1, 2, False)

            branch(pe, fast, general)

        @block.scalar
        def _(act):
            def h_relu(part):
                end = sum(PARTS[:part + 1])
                act.wait_ge(S.ln_ready, 1 + [sum(NORM_PARTS[:q + 1]) >= end for q in range(len(NORM_PARTS))].index(True))
                relu_blocks(act, sum(PARTS[:part]), PARTS[part], lambda j: node_b[:, j * D:(j + 1) * D]).then_inc(hy_ready, 1)

            def a_sum(t, par, first):
                act.wait_ge(unit_mm, (t + 1) * UC)
                if not first:
                    act.wait_ge(S.nT_ready, t)
                nc.scalar.mul(lo_sum[:, :], lo_ps[par][:, :], 1 / (ONE * H_SCALE * LO)).then_inc(lo_ready, 1)

            def a_sig(t):
                act.wait_ge(S.zb_ready, t + 1)
                nc.scalar.activation(sig[:, :], zb[:, :], ACT.Sigmoid).then_inc(S.sig_ready, 1)

            def job_low(now, k):
                act.wait_ge(job_used, now.pairs_before + now.pairs.index((k, len(now.jobs[k][1]) // 2 - 1)) + 1)
                if not (now.first and k == 0):
                    act.wait_ge(part_out, 16 * (now.before + k))
                nc.scalar.activation(job_sum, job_lo_ps[:, :], ACT.Identity, scale=alpha1[:, 1:2]).then_inc(job_lo_ready, 1)

            def job_store(now, k):
                act.wait_ge(job_sum_ready, now.before + k + 1)
                act.dma_start(part_v[:, bass.ds(now.jobs[k][2], 1), :].rearrange("p o n -> p (o n)"), job_sum).then_inc(part_out, 16)

            def first_pass(turn, least):
                first = least == 0
                now = Turn(turn, least) if least >= FIRST_JOB_TURN else None
                for par in range(2):
                    c = turn * 2 + par
                    if first and par == 0:
                        h_relu(0)
                    for u in range(UC):
                        if first and par == 0 and u in H_RELU_AT:
                            h_relu(H_RELU_AT[u])
                        for i in (2 * u, 2 * u + 1):
                            act.wait_ge(tile_in[i % RING], 16 * (c * (TC // RING) + i // RING + 1))
                            if not (first and par == 0 and i == 0):
                                act.wait_ge(counted, c * TC + i)
                            nc.scalar.activation(unused[:, :], slot(i).bitcast(U32), ACT.Sign,
                                                 accum_out=nz_count[:, bass.ds(c * TC + i, 1)]).then_inc(counted, 1)
                        if not (first and par == 0):
                            if u == 1:
                                a_sum(c - 1, 1 - par, first)
                            elif u == 3:
                                a_sig(c - 1)
                            elif u == 4:
                                high_part(act, c - 1, c - 1, node_b16)
                            elif u == 5:
                                low_part(act, S, c - 1, c - 1, node_b16)
                        if now:
                            after = par * UC + u
                            if after - 1 in now.low_at:
                                job_store(now, now.low_at[after - 1])
                            if after in now.low_at:
                                job_low(now, now.low_at[after])
                if now and 2 * UC - 1 in now.low_at:
                    job_store(now, now.low_at[2 * UC - 1])
            chunks(act, first_pass, FIRST)
            a_sum(NC - 1, 1, False)

            def fast():
                job_low(last_turn, len(last_turn.jobs) - 1)
                a_sig(NC - 1)
                job_store(last_turn, len(last_turn.jobs) - 1)
                high_part(act, NC - 1, NC - 1, node_b16)
                low_part(act, S, NC - 1, NC - 1, node_b16)
                for p in (1, 2):
                    chunks(act, lambda turn, least: [finish_act(act, S, turn, par, p, least == 0, True, jobs_had(p, least, par)) for par in range(2)],
                           SECOND if p == 1 else (1,))
                store_end(act, S)

            def general():
                for q in range(4):
                    act.wait_ge(G.ln_ready, q + 1)
                    relu_blocks(act, q * 16, 16, lambda j: node_a[:, j * D:(j + 1) * D]).then_inc(G.h_ready, 1)
                for p in range(3):
                    chunks(act, lambda turn, least: [finish_act(act, G, turn, par, p, least == 0, False) for par in range(2)])
                store_end(act, G)

            branch(act, fast, general)

        @block.vector
        def _(dve):
            nc.vector.memset(ones[:, :], 1.0).then_inc(ones_set, 1)
            nc.vector.memset(ones16[:, :], 1.0).then_inc(ones_set, 1)
            nc.vector.memset(first_row[:, :], 0.0).then_inc(row_zero, 1)
            dve.wait_ge(row_zero, 1)
            nc.vector.memset(first_row[0:1, :], 1.0).then_inc(ones_set, 1)
            first_norm(dve, S, x_in[0], 0, 0, NORM_PARTS[0], H_SCALE)
            dve.wait_ge(w_in, 64)
            nc.vector.tensor_tensor(wsq, w_sb[:, 0:D], w_sb[:, 0:D], ALU.mult).then_inc(wsq_ready, 1)

            def feature_scales():
                link = chain(dve, bound_step, 0)
                dve.wait_ge(wsum_done, 1)
                link(nc.vector.tensor_scalar(wsq, z_ps[:, 0:D], 1e-30, None, ALU.add))
                rsqrt(nc, link, wsq, bound, wtmp)
                link(nc.vector.tensor_tensor(bound, bound, wsq, ALU.mult))
                link(nc.vector.scalar_tensor_tensor(wtmp, b_sb[:, 0:D], -1.0, b_sb[:, 0:D], ALU.mult, ALU.max))
                link(nc.vector.scalar_tensor_tensor(bound, bound, SUM_BOUND, wtmp, ALU.mult, ALU.add))
                link(nc.vector.tensor_scalar(bound, bound, 1e-18, None, ALU.max))
                link(nc.vector.tensor_scalar(bound.bitcast(I32), bound.bitcast(I32), 0x7F800000, None, ALU.bitwise_and))
                nc.vector.tensor_scalar(s_row[:, :].bitcast(I32), bound.bitcast(I32), -1.0, float((127 + 127 + 14) << 23),
                                        ALU.mult, ALU.add).then_inc(s_ready, 1)
                link = chain(dve, alpha_step, 0)
                dve.wait_ge(s_col_done, 1)
                link(nc.vector.tensor_copy(alpha1[:, 0:1], misc_ps[:, 0:1]))
                link(nc.vector.tensor_scalar(alpha1[:, 0:1].bitcast(I32), alpha1[:, 0:1].bitcast(I32), -1.0, float((127 + 127 - 1) << 23),
                                             ALU.mult, ALU.add))
                link(nc.vector.tensor_scalar(alpha1[:, 1:2], alpha1[:, 0:1], 1 / LO, None, ALU.mult))

            def v_sum(t, par, first):
                dve.wait_ge(lo_ready, t + 1)
                nc.vector.scalar_tensor_tensor(half(nT, par), hi_ps[par][:, :], 1 / (ONE * H_SCALE), lo_sum[:, :],
                                               ALU.mult, ALU.add).then_inc(S.nT_ready, 1)

            def v_bias(t):
                dve.wait_ge(S.z_done, t + 1)
                nc.vector.tensor_tensor(b3(zb[:, :]), b3(z_ps[:, :]), bias(0), ALU.add).then_inc(S.zb_ready, 1)
                dve.wait_ge(S.dcol_done, t + 1)
                nc.vector.tensor_scalar(deg[:, bass.ds(t * CB, CB)], misc_ps[:, 0:CB], 1.0, None, ALU.add).then_inc(S.deg_done, 1)

            def count_ones(c, par, part):
                link = chain(dve, count_step, COUNT_STEPS * c + part * (COUNT_STEPS // 2))
                src = bits[:, bass.ds((c * UC + part * (UC // 2)) * WORDS, UC // 2 * WORDS)]
                n2, n1 = 2 * WORDS, WORDS
                a, b = count_a, half(nT, par).bitcast(U32)

                def fields(out, x, shift, mask):
                    if shift:
                        link(nc.vector.tensor_scalar(out, x, shift, mask, ALU.logical_shift_right, ALU.bitwise_and))
                    else:
                        link(nc.vector.tensor_scalar(out, x, mask, None, ALU.bitwise_and))

                def plus(out, x, z, op=ALU.add):
                    link(nc.vector.tensor_tensor(out.bitcast(U16), x.bitcast(U16), z.bitcast(U16), op))
                fields(a, src, 1, 0x55555555)
                plus(b, src, a, ALU.subtract)
                fields(a, b, 2, 0x33333333)
                fields(b, b, 0, 0x33333333)
                plus(a, a, b)
                plus(a[:, 0:n2], a[:, 0:n2], a[:, n2:2 * n2])
                fields(b[:, 0:n2], a[:, 0:n2], 4, 0x0F0F0F0F)
                fields(a[:, 0:n2], a[:, 0:n2], 0, 0x0F0F0F0F)
                plus(a[:, 0:n2], a[:, 0:n2], b[:, 0:n2])
                if part == 0:
                    plus(count8, a[:, 0:n1], a[:, n1:n2])
                    link(nc.vector.tensor_copy(a[:, 0:n1], count8))
                else:
                    plus(a[:, 0:n1], a[:, 0:n1], a[:, n1:n2])
                    plus(count8, count8, a[:, 0:n1])

            def count_columns(c, first):
                if not first:
                    dve.wait_ge(S.dcol_done, c)
                nc.vector.tensor_scalar(count16[:, :], count8.bitcast(U8), 1.0, None, ALU.mult, ALU.add,
                                        accum_out=one_count[:, bass.ds(c, 1)]).then_inc(counted16, 1)

            def job_unpack(now, m):
                k, i = now.pairs[m]
                n, units, _ = now.jobs[k]
                if not (now.first and m == 0):
                    dve.wait_ge(job_used, now.pairs_before + m)
                src = bits[:, bass.ds((n * UC + units[2 * i]) * WORDS, 2 * WORDS)].rearrange("p (g w) -> p g w", g=2)
                dst = job_slot[:, :].bitcast(U32).rearrange("p (g k w) -> p g k w", g=2, k=UB)
                for b in range(UB):
                    last = unpack_bit(dst[:, :, b, :], src, b)
                last.then_inc(job_unpacked, 1)

            def job_join(now, k):
                dve.wait_ge(job_lo_ready, now.before + k + 1)
                nc.vector.scalar_tensor_tensor(job_sum, job_hi_ps[:, :], alpha1[:, 0:1], job_sum,
                                               ALU.mult, ALU.add).then_inc(job_sum_ready, 1)

            def halve_again(g):
                dve.wait_ge(pack4_ready, g + 1)
                nc.vector.scalar_tensor_tensor(pack2, pack4[:, 0:2 * WORDS], 2, pack4[:, 2 * WORDS:4 * WORDS],
                                               ALU.logical_shift_right, ALU.bitwise_or).then_inc(pack2_ready, 1)

            def pack_last(g):
                dve.wait_ge(pack2_ready, g + 1)
                nc.vector.scalar_tensor_tensor(bits[:, bass.ds(g * WORDS, WORDS)], pack2[:, 0:WORDS], 4, pack2[:, WORDS:2 * WORDS],
                                               ALU.logical_shift_right, ALU.bitwise_or).then_inc(bits_ready, 1)

            def first_pass(turn, least):
                first = least == 0
                now = Turn(turn, least) if least >= FIRST_JOB_TURN else None
                if now:
                    dve.wait_ge(bits_ready, 2 * turn * UC)
                for par in range(2):
                    c = turn * 2 + par
                    for u in range(UC):
                        if first and par == 0 and u in NORM_AT:
                            q = NORM_AT[u]
                            first_norm(dve, S, x_in[q], q, sum(NORM_PARTS[:q]), NORM_PARTS[q], H_SCALE)
                        g = c * UC + u
                        if not (first and par == 0 and u < 2):
                            dve.wait_ge(unit_mm, g - 1)
                        m = marks[:, (u % 2) * UB * CW:(u % 2 + 1) * UB * CW]
                        deferred = u % (UC // 2) > 0
                        for i in range(2):
                            dve.wait_ge(tile_in[(2 * u + i) % RING], 16 * (c * (TC // RING) + (2 * u + i) // RING + 1))
                            nc.vector.tensor_scalar(m[:, i * TB * CW:(i + 1) * TB * CW], slot(2 * u + i), 1.0, float(ONE_BYTE),
                                                    ALU.is_equal, ALU.mult).then_inc(marked, 1)
                            if deferred:
                                (halve_again, pack_last)[i](g - 1)
                        m32 = m.bitcast(U32)
                        dve.wait_ge(marked, 2 * g + 2)
                        nc.vector.scalar_tensor_tensor(pack4, m32[:, 0:4 * WORDS], 1, m32[:, 4 * WORDS:8 * WORDS],
                                                       ALU.logical_shift_left, ALU.bitwise_or).then_inc(pack4_ready, 1)
                        if u % (UC // 2) == UC // 2 - 1:
                            halve_again(g)
                            pack_last(g)
                        if not (first and par == 0):
                            if u == 1:
                                v_sum(c - 1, 1 - par, first)
                            elif u == 3:
                                v_bias(c - 1)
                        if first and par == 0 and u == SCALES_AT:
                            feature_scales()
                        if now:
                            after = par * UC + u
                            if after in now.low_at:
                                job_join(now, now.low_at[after])
                            if after in now.pair_at:
                                job_unpack(now, now.pair_at[after])
                        if u == UC // 2 - 1:
                            dve.wait_ge(bits_ready, g + 1)
                            count_ones(c, par, 0)
                        elif u == 0 and not (first and par == 0):
                            dve.wait_ge(bits_ready, g)
                            count_ones(c - 1, 1 - par, 1)
                            count_columns(c - 1, first and par == 1)
            chunks(dve, first_pass, FIRST)
            dve.wait_ge(bits_ready, NC * UC)
            count_ones(NC - 1, 1, 1)
            count_columns(NC - 1, False)

            dve.wait_ge(counted, NC * TC)
            link = chain(dve, flag_step, 0)
            link(nc.vector.tensor_reduce(nz_chunk[:, :], nz_count[:, :].rearrange("p (c i) -> p c i", i=TC), AX.X, ALU.add))
            dve.wait_ge(counted16, NC)
            link(nc.vector.tensor_tensor(differ[:, :], nz_chunk[:, :], one_count[:, :], ALU.not_equal))
            nc.vector.tensor_reduce(flag_f[:, :], differ[:, :], AX.X, ALU.max).then_inc(differ_ready, 1)
            v_sum(NC - 1, 1, False)
            dve.wait_ge(differ_sum, 1)
            nc.vector.tensor_scalar(flag[:, :], misc_ps[:, CB:CB + 1], 0.0, None, ALU.is_gt).then_inc(flag_ready, 1)

            def fast():
                def unpack(c, v, had, par, a=0, b=GC):
                    for k, (gq, where) in [*enumerate(slots(had, par))][a:b]:
                        n = first_slot(v, not had) + k
                        if not (isinstance(n, int) and n < RING):
                            dve.wait_ge(slot_used, n - RING + 1)
                        src = bits[:, bass.ds((c * GC + gq) * GB * WORDS, GB * WORDS)].rearrange("p (g w) -> p g w", g=GB)
                        dst = slot(where).bitcast(U32).rearrange("p (g k w) -> p g k w", g=GB, k=UB)
                        for block_ in range(UB):
                            last = unpack_bit(dst[:, :, block_, :], src, block_)
                        last.then_inc(unpacked, 1)

                dve.wait_ge(bits_ready, NC * UC)
                unpack(0, 0, True, 0)
                unpack(1, 1, True, 1, 0, 1)
                job_join(last_turn, len(last_turn.jobs) - 1)
                v_bias(NC - 1)
                dve.wait_ge(S.deg_done, NC)
                rsqrt(nc, chain(dve, S.dinv_step, 0), deg[:, :], dinv[:, :], tmp[:, :])
                for p in (1, 2):
                    def body(turn, least):
                        first = least == 0
                        for par in range(2):
                            c = turn * 2 + par
                            last = isinstance(turn, int) and turn == NC // 2 - 1 and par == 1
                            if last and p == 1:
                                unpack(0, NC, False, 0)
                            elif not last:
                                unpack(c + 1, c + NC * (p - 1) + 1, jobs_had(p, least + par, 1 - par), 1 - par,
                                       1 if jobs_had(p, least, par) else 0)
                            meanwhile = None
                            if jobs_had(p, least + par, 1 - par):
                                def meanwhile(c=c, par=par):
                                    unpack(c + 2, c + 2, jobs_had(p, least + 1, par), par, 0, 1)
                            finish_dve(dve, S, turn, par, p, first, True, jobs_had(p, least, par), meanwhile)
                    chunks(dve, body, SECOND if p == 1 else (1,), peel_last=True)

            def general():
                for q in range(4):
                    first_norm(dve, G, g_x_in[q], q, q * 16, 16, 1.0)
                for p in range(3):
                    def body(turn, least):
                        first = least == 0
                        for par in range(2):
                            c = turn * 2 + par
                            if p == 0:
                                acc = half(degacc, par)
                                for i in range(TC):
                                    g = c * TC + i
                                    dve.wait_ge(g_tile_in[i % RING], 16 * (c * (TC // RING) + i // RING + 1))
                                    if i == 0 and not first:
                                        dve.wait_ge(G.dcol_done, c - 1)
                                    til = slot(i).rearrange("p (q n) -> p n q", q=TB)
                                    nc.vector.tensor_reduce(acc if i == 0 else degtile, til, AX.X, ALU.add).then_inc(g_tile_red, 1)
                                    dve.wait_ge(g_tile_red, g + 1)
                                    if i > 0:
                                        last = nc.vector.tensor_tensor(acc, acc, degtile, ALU.add)
                                        last.then_inc(g_degacc_done if i == TC - 1 else g_degstep, 1)
                                        if i < TC - 1:
                                            dve.wait_ge(g_degstep, c * (TC - 2) + i)
                                dve.wait_ge(G.z_done, c + 1)
                                nc.vector.tensor_tensor(b3(zb[:, :]), b3(z_ps[:, :]), bias(0), ALU.add).then_inc(G.zb_ready, 1)
                                dve.wait_ge(G.dcol_done, c + 1)
                                nc.vector.tensor_scalar(deg[:, bass.ds(c * CB, CB)], misc_ps[:, 0:CB], 1.0, None, ALU.add).then_inc(G.deg_done, 1)
                                dve.wait_ge(G.sig_ready, c + 1)
                                nc.vector.tensor_tensor(blocks(node_b, c * CB, CB), zb[:, :], sig[:, :], ALU.mult).then_inc(G.node_ready, 1)
                            else:
                                finish_dve(dve, G, turn, par, p, first, False)
                    chunks(dve, body)
                    if p == 0:
                        dve.wait_ge(G.deg_done, NC)
                        link = chain(dve, G.dinv_step, 0)
                        rsqrt(nc, link, deg[:, :], dinv[:, :], tmp[:, :])
                        link(nc.vector.tensor_tensor(dinv[:, :], dinv[:, :], deg[:, :], ALU.mult))
                        link(nc.vector.reciprocal(dinv[:, :], dinv[:, :]))
                        link(nc.vector.tensor_scalar(tmp[:, :], deg[:, :], 0.0, HUGE, ALU.is_lt, ALU.mult))
                        link(nc.vector.tensor_scalar(tmp[:, :], tmp[:, :], HUGE, None, ALU.mult))
                        link(nc.vector.tensor_tensor(tmp[:, :], tmp[:, :], tmp[:, :], ALU.subtract))
                        link(nc.vector.tensor_tensor(dinv[:, :], dinv[:, :], tmp[:, :], ALU.add))

            branch(dve, fast, general)


def kernel(x, adj, L0_gnn_W, L0_gnn_b, L1_gnn_W, L1_gnn_b):
    import concourse.bacc as bacc
    from concourse.bass_utils import run_bass_kernel_spmd

    nc = bacc.Bacc("TRN2", target_bir_lowering=False, num_devices=1, dynamic_dma_scratch_size=1024)
    tiles = np.asarray(adj).reshape(NC, CW, TC, TB, P).transpose(0, 2, 4, 3, 1)
    arrays = {
        "x": np.ascontiguousarray(x),
        "adj": np.ascontiguousarray(tiles).reshape(NC * TC * P, TB * CW),
        "w0": np.ascontiguousarray(L0_gnn_W),
        "b0": np.ascontiguousarray(L0_gnn_b).reshape(1, D),
        "w1t": np.ascontiguousarray(np.asarray(L1_gnn_W).T),
        "b1": np.ascontiguousarray(L1_gnn_b).reshape(1, D),
    }
    args = [nc.dram_tensor(k, a.shape, mybir.dt.from_np(a.dtype), kind="ExternalInput").ap() for k, a in arrays.items()]
    out = nc.dram_tensor("out", (N, D), F32, kind="ExternalOutput").ap()
    program(nc, *args, out)
    r = run_bass_kernel_spmd(nc, [arrays], core_ids=[0])
    return r.results[0]["out"]
```
